# Optimizing a Trainium2 kernel written in Bass

```python
import numpy as np
import jax
import jax.numpy as jnp

def _softmax(x, axis=-1):
    return jax.nn.softmax(x, axis=axis)

def _gelu(x):
    return jax.nn.gelu(x, approximate=True)

def _silu(x):
    return jax.nn.silu(x)

def _sigmoid(x):
    return jax.nn.sigmoid(x)

def _layernorm(x, axis=-1, eps=1e-05):
    m = jnp.mean(x, axis=axis, keepdims=True)
    v = jnp.var(x, axis=axis, keepdims=True)
    return (x - m) / jnp.sqrt(v + eps)

def _scatter_add(tgt, idx, src, axis=0):
    return tgt.at[idx].add(src)

def _segment_sum(src, seg, n):
    return jax.ops.segment_sum(src, seg, n)
kernel_name = 'mk_xattn_ffn_d1_seqx_r4_8181a1'

def setup_inputs(seed: int=0):
    np.random.seed(seed)
    _w = jnp.asarray

    def _rec_inputs():
        import jax
        import jax.numpy as jnp
        _rk = jax.random.key(seed)
        x = 7.22e-05 + 1 * jax.random.normal(jax.random.fold_in(_rk, 1), (2, 512, 512), jnp.float32)
        _lenS = 512 - jax.random.randint(jax.random.fold_in(_rk, 7), (2,), 0, max(1, 512 // 4) + 1, jnp.int32)
        _lenS2 = 1024 - jax.random.randint(jax.random.fold_in(_rk, 8), (2,), 0, max(1, 1024 // 4) + 1, jnp.int32)
        _ctx_2048P = jax.random.normal(jax.random.fold_in(_rk, 11), (2, 16, 512), jnp.float32)
        _ctx_2048c = jax.random.dirichlet(jax.random.fold_in(_rk, 511), 0.3 * jnp.ones((16,), jnp.float32), (2, 1024))
        _ctx_2048t = jnp.einsum('bsk,bkd->bsd', _ctx_2048c, _ctx_2048P)
        _ctx_2048t = _ctx_2048t * jax.lax.rsqrt(jnp.mean(jnp.square(_ctx_2048t)) + 1e-12) * 0.953939
        ctx_2048 = 4.13588e-05 + 0.999923 * (_ctx_2048t + 0.3 * jax.random.normal(jax.random.fold_in(_rk, 611), (2, 1024, 512), jnp.float32))
        return (x, ctx_2048)
    x, ctx_2048 = _rec_inputs()

    def _L0_xattn_setup():
        import math
        import jax, jax.numpy as jnp
        import numpy as np
        HEADS = 16
        MASKED_BIAS = -10000.0

        def _mha(q, k, v):
            B, Sq, D = q.shape
            Sk = k.shape[-2]
            hd = D // HEADS
            qh = q.reshape(B, Sq, HEADS, hd).transpose(0, 2, 1, 3)
            kh = k.reshape(B, Sk, HEADS, hd).transpose(0, 2, 1, 3)
            vh = v.reshape(B, Sk, HEADS, hd).transpose(0, 2, 1, 3)
            scores = jnp.einsum('bhqd,bhkd->bhqk', qh, kh) / math.sqrt(hd)
            qi = jnp.arange(Sq)[:, None] + (Sk - Sq)
            ki = jnp.arange(Sk)[None, :]
            causal = ki <= qi
            scores = jnp.where(causal[None, None], scores, jnp.asarray(MASKED_BIAS, scores.dtype))
            attn = jax.nn.softmax(scores, axis=-1)
            out = jnp.einsum('bhqk,bhkd->bhqd', attn, vh)
            return out.transpose(0, 2, 1, 3).reshape(B, Sq, D)
        key = jax.random.key(seed)
        kq, kk, kv = jax.random.split(key, 3)
        B, S, D = (4, 256, 512)
        q = jax.random.normal(kq, (B, S, D), dtype=jnp.float32)
        k = jax.random.normal(kk, (B, S, D), dtype=jnp.float32)
        v = jax.random.normal(kv, (B, S, D), dtype=jnp.float32)
        return {'q': q, 'k': k, 'v': v}
    _L0_xattn_all = _L0_xattn_setup()
    _L0_xattn_in = {k: v for k, v in _L0_xattn_all.items() if k in ()}
    del _L0_xattn_all

    def _L0_ffn_setup():
        import jax, jax.numpy as jnp
        import numpy as np
        N, S, D = (8, 512, 512)
        O = 512
        E = 8
        K = 2
        key = jax.random.key(seed)
        ks = jax.random.split(key, 5)
        scale_in = 1.0 / np.sqrt(D)
        x = jax.random.normal(ks[0], (N, S, D), dtype=jnp.float32)
        gate_w = jax.random.uniform(ks[1], (D, E), dtype=jnp.float32, minval=-scale_in, maxval=scale_in)
        gate_b = jax.random.uniform(ks[2], (E,), dtype=jnp.float32, minval=-scale_in, maxval=scale_in)
        expert_w = jax.random.uniform(ks[3], (E, D, O), dtype=jnp.float32, minval=-scale_in, maxval=scale_in)
        expert_b = jax.random.uniform(ks[4], (E, O), dtype=jnp.float32, minval=-scale_in, maxval=scale_in)
        return {'x': x, 'gate_w': gate_w, 'gate_b': gate_b, 'expert_w': expert_w, 'expert_b': expert_b}
    _L0_ffn_all = _L0_ffn_setup()
    _L0_ffn_in = {k: v for k, v in _L0_ffn_all.items() if k in ('gate_w', 'gate_b', 'expert_w', 'expert_b')}
    del _L0_ffn_all
    return {'x': x, 'ctx_2048': ctx_2048, 'L0_ffn_gate_w': _L0_ffn_in['gate_w'], 'L0_ffn_gate_b': _L0_ffn_in['gate_b'], 'L0_ffn_expert_w': _L0_ffn_in['expert_w'], 'L0_ffn_expert_b': _L0_ffn_in['expert_b']}

def reference(x, ctx_2048, L0_ffn_gate_w, L0_ffn_gate_b, L0_ffn_expert_w, L0_ffn_expert_b):
    import jax
    import jax.numpy as jnp

    def _L0_xattn_ref(q, k, v):
        import math
        import jax, jax.numpy as jnp
        import numpy as np
        HEADS = 16
        MASKED_BIAS = -10000.0

        def _mha(q, k, v):
            B, Sq, D = q.shape
            Sk = k.shape[-2]
            hd = D // HEADS
            qh = q.reshape(B, Sq, HEADS, hd).transpose(0, 2, 1, 3)
            kh = k.reshape(B, Sk, HEADS, hd).transpose(0, 2, 1, 3)
            vh = v.reshape(B, Sk, HEADS, hd).transpose(0, 2, 1, 3)
            scores = jnp.einsum('bhqd,bhkd->bhqk', qh, kh) / math.sqrt(hd)
            qi = jnp.arange(Sq)[:, None] + (Sk - Sq)
            ki = jnp.arange(Sk)[None, :]
            causal = ki <= qi
            scores = jnp.where(causal[None, None], scores, jnp.asarray(MASKED_BIAS, scores.dtype))
            attn = jax.nn.softmax(scores, axis=-1)
            out = jnp.einsum('bhqk,bhkd->bhqd', attn, vh)
            return out.transpose(0, 2, 1, 3).reshape(B, Sq, D)
        return _mha(q, k, v)

    def _L0_ffn_ref(x, gate_w, gate_b, expert_w, expert_b):
        import jax, jax.numpy as jnp
        import numpy as np
        N, S, D = (8, 512, 512)
        O = 512
        E = 8
        K = 2
        gate_logits = jnp.einsum('nsd,de->nse', x, gate_w) + gate_b
        _, top_idx = jax.lax.top_k(gate_logits, K)
        all_out = jax.nn.relu(jnp.einsum('nsd,edo->nseo', x, expert_w) + expert_b)
        sel = jnp.take_along_axis(all_out, top_idx[..., None], axis=2)
        return sel.mean(axis=2)
    x = x + _L0_xattn_ref(_layernorm(x, axis=-1), ctx_2048, ctx_2048)
    x = x + _L0_ffn_ref(_layernorm(x, axis=-1), L0_ffn_gate_w, L0_ffn_gate_b, L0_ffn_expert_w, L0_ffn_expert_b)
    return x

_drawn_inputs = setup_inputs


def setup_inputs(seed=0):
    import zlib

    import numpy as np

    out = dict(_drawn_inputs(seed))
    spreads = {}
    factors = {'L0_ffn_expert_b': 5.791}
    for name, (base, spread) in spreads.items():
        noise = np.random.default_rng([zlib.crc32(name.encode()), seed]).standard_normal(out[name].shape)
        drawn = base * np.exp(spread * noise) if base else spread * noise
        out[name] = jnp.asarray(drawn.astype(out[name].dtype))
    for name, factor in factors.items():
        out[name] = (out[name] * factor).astype(out[name].dtype)
    return out
```

```python
import concourse.bass as bass
from concourse import mybir
from contextlib import ExitStack

F32 = mybir.dt.float32
F32R = mybir.dt.float32r
BF16 = mybir.dt.bfloat16
U32 = mybir.dt.uint32
ALU = mybir.AluOpType
ACT = mybir.ActivationFunctionType
AX = mybir.AxisListType

P = 128
HEADS = 16
NEG = -1e30
EPS = 1e-5


def bass_cross_attention_moe(nc, x, x_T, ctx, ctx_T, gate_w, gate_b, expert_w, expert_b, out):
    B, SQ, D = x.shape
    SK = ctx.shape[1]
    E = gate_w.shape[1]
    HD = D // HEADS
    HG = P // HD
    NG = D // P
    N = B * NG
    QT = SQ // P
    KT = SK // P
    T = B * QT
    KC = D // P
    SCALE = float(HD) ** -0.5
    ROWS = 3 * HD
    R = 3
    NP = 2
    SPLITS = 6
    MAXU = HG * QT
    UNITS = MAXU + 2
    COPIES = 3 * HG
    ROUND = [0] + list(range(KT - QT + 1, KT)) + list(range(1, KT - QT + 1))
    LOOPS = (N - 2) // R
    assert HD == 32 and HG == 4 and SQ == 512 and SK == 1024 and (N - 2) % R == 0 and UNITS % 2 == 0

    def q_from(c):
        return max(0, c - (KT - QT)) * P

    def at(i, r, k):
        return i + (r + k) // R, (r + k) % R

    def first_unit(i, r):
        return UNITS * (R * i + r + 1)

    def slot(pos):
        return pos % 2

    PLAN = [3, 2, 2, 2, 3, 3, 2, 0]

    def plan():
        units = [("max", m) for m in range(MAXU)] + [("turn", 0)]
        rounds, k = [], 0
        for c in PLAN:
            rounds.append([(k + d, *u) for d, u in enumerate(units[k:k + c])])
            k += c
        assert k == len(units)
        return rounds

    outer = ExitStack()
    with outer:
        def tensor(stack, name, shape, dt=F32):
            return stack.enter_context(nc.sbuf_tensor(name, shape, dt))

        def sem(name):
            return outer.enter_context(nc.semaphore(name))

        def sems(name):
            return [sem(f"{name}{r}") for r in range(R)]

        ident = tensor(outer, "ident", [P, P])
        identb = tensor(outer, "identb", [P, P], BF16)
        mask_qk = tensor(outer, "mask_qk", [P, P], BF16)
        mask_kq = tensor(outer, "mask_kq", [P, P], BF16)
        ones = tensor(outer, "ones", [P, P])
        attnT = tensor(outer, "attnT", [P, N, SQ])
        stats = tensor(outer, "stats", [P, T, 6])
        mv = tensor(outer, "mv", [P, T, 2])
        std = tensor(outer, "std", [P, T])
        rstd = tensor(outer, "rstd", [P, T])
        nmr = tensor(outer, "nmr", [P, T])
        eps = tensor(outer, "eps", [P, 1])
        x1 = tensor(outer, "x1", [P, T, D])
        W = tensor(outer, "W", [P, 2, KC, D])
        gw = tensor(outer, "gw", [P, KC, E])
        gb = tensor(outer, "gb", [P, E])
        iota = tensor(outer, "iota", [P, E])

        inner = ExitStack()
        rstd_row = tensor(inner, "rstd_row", [P, T, P])
        nmr_row = tensor(inner, "nmr_row", [P, T, P])
        diag = tensor(inner, "diag", [P, 2, P])
        k_raw = tensor(inner, "k_raw", [P, R, SK])
        x_raw = tensor(inner, "x_raw", [P, R, SQ])
        val = tensor(inner, "val", [P, R, KT, P])
        k_hi = tensor(inner, "k_hi", [P, SK], F32R)
        k_lo = tensor(inner, "k_lo", [P, SK], F32R)
        qn = tensor(inner, "qn", [P, SQ])
        q_hi = tensor(inner, "q_hi", [P, SQ], F32R)
        q_lo = tensor(inner, "q_lo", [P, SQ], F32R)
        kst = tensor(inner, "kst", [P, R, HG, SK], F32R)
        qst = tensor(inner, "qst", [P, R, HG, SQ], F32R)
        mx = tensor(inner, "mx", [P, P])
        mrow = tensor(inner, "mrow", [MAXU, P], F32R)
        prob = tensor(inner, "prob", [P, NP, HG, SQ])
        rden = tensor(inner, "rden", [P, SQ])
        inner.close()

        late = ExitStack()
        xn2 = tensor(late, "xn2", [P, T, D])
        xT = tensor(late, "xT", [P, T, KC, P])
        eb = tensor(late, "eb", [P, E, D])
        logit = tensor(late, "logit", [P, T, E])
        top = tensor(late, "top", [P, T, 8])
        topi = tensor(late, "topi", [P, T, 8], U32)
        topf = tensor(late, "topf", [P, T, 8])
        hot = tensor(late, "hot", [P, T, E])
        hot2 = tensor(late, "hot2", [P, T, E])
        wsel = tensor(late, "wsel", [P, T, E])
        hid = tensor(late, "hid", [P, 2, D])
        relu = tensor(late, "relu", [P, 2, D])
        late.close()

        ring = [outer.enter_context(nc.psum_tensor(f"ring{s}", [P, 2 * 512], F32)) for s in range(2)]
        sc = [outer.enter_context(nc.psum_tensor(f"sc{s}", [P, 512], F32)) for s in range(2)]
        num = outer.enter_context(nc.psum_tensor("num", [P, 512], F32))
        den = outer.enter_context(nc.psum_tensor("den", [P, 512], F32))
        banks = [ring[0][:, 0:512], ring[0][:, 512:1024], ring[1][:, 0:512], ring[1][:, 512:1024],
                 sc[0][:, :], sc[1][:, :], num[:, :], den[:, :]]

        ROW_BANK = ((6, 7), (4, 5))

        SC_CREDIT, PV_CREDIT, OUT_CREDIT = 2, NP, 1
        const0 = sem("const0")
        const = sem("const")
        one_in = sem("one_in")
        x_in = [sem(f"x_in{t}") for t in range(T)]
        stat_done = sem("stat_done")
        std_done = sem("std_done")
        diag_done = sem("diag_done")
        row_full = sem("row_full")
        row_done = sem("row_done")
        kraw_in, xraw_in, val_in = sems("kraw_in"), sems("xraw_in"), sems("val_in")
        split_done = sem("split_done")
        kst_in, qst_in, max_in = sems("kst_in"), sems("qst_in"), sems("max_in")
        ring_full = sem("ring_full")
        ring_free = sem("ring_free")
        sc_full = sem("sc_full")
        exp_done = sem("exp_done")
        pv_done = sem("pv_done")
        rec_done = sem("rec_done")
        out_done = sem("out_done")
        gate_in = sem("gate_in")
        bias_in = sem("bias_in")
        back_full = sem("back_full")
        post = sem("post")
        norm2_done = sem("norm2_done")
        turn_full = sem("turn_full")
        turn_done = sem("turn_done")
        gate_full = sem("gate_full")
        w_in = [sem("w_in0"), sem("w_in1")]
        y_full = sem("y_full")
        hid_done = sem("hid_done")
        relu_done = sem("relu_done")
        acc_done = sem("acc_done")
        stored = sem("stored")

        x_tiles = x.rearrange("b (t p) d -> p (b t) d", p=P)
        out_tiles = out.rearrange("b (t p) d -> p (b t) d", p=P)

        block = outer.enter_context(nc.Block())

        @block.sync
        def _(sp):
            def stack(r, split_k, split_q):
                sp.wait_ge(split_done, split_k)
                for to, half in ((0, k_hi), (1, k_hi), (2, k_lo)):
                    for j in range(HG):
                        sp.dma_start(kst[to * HD:(to + 1) * HD, r, j, :].bitcast(F32),
                                     half[j * HD:(j + 1) * HD, :].bitcast(F32)).then_inc(kst_in[r], 16)
                sp.wait_ge(split_done, split_q)
                for to, half in ((0, q_hi), (1, q_lo), (2, q_hi)):
                    for j in range(HG):
                        sp.dma_start(qst[to * HD:(to + 1) * HD, r, j, :].bitcast(F32),
                                     half[j * HD:(j + 1) * HD, :].bitcast(F32)).then_inc(qst_in[r], 16)

            def send_max(r, taken):
                sp.wait_ge(ring_free, taken)
                sp.dma_start(qst[ROWS:ROWS + 1, r].bitcast(F32).rearrange("o j (t q) -> o (j t) q", q=P),
                             mrow[:, :].bitcast(F32)).then_inc(max_in[r], 16)

            def step(i, r, prep=True):
                n = R * i + r
                if prep:
                    stack((r + 2) % R, SPLITS * (n + 2) + 2, SPLITS * (n + 3))
                send_max((r + 1) % R, UNITS * (n + 2))

            def load(to, group_of, n, done):
                sp.dma_start(to, group_of[n]).then_inc(done, 16)

            load(k_raw[:, 0], ctx_T, 0, kraw_in[0])
            for t in range(T):
                sp.dma_start(x1[:, t], x_tiles[:, t]).then_inc(x_in[t], 16)
                if t == QT - 1:
                    load(x_raw[:, 0], x_T, 0, xraw_in[0])
            load(k_raw[:, 1], ctx_T, 1, kraw_in[1])
            load(x_raw[:, 1], x_T, 1, xraw_in[1])
            sp.dma_start(val[:, 0], ctx[0].rearrange("(c p) d -> p c d", p=P)).then_inc(val_in[0], 16)
            sp.wait_ge(const0, 7)
            for r in range(R):
                sp.dma_start(kst[ROWS:ROWS + 1, r].bitcast(F32).rearrange("o j (t k) -> o (j t) k", k=P),
                             ones[0:HG * KT, :]).then_inc(one_in, 16)
            stack(0, 2, SPLITS)
            stack(1, SPLITS + 2, 2 * SPLITS)
            send_max(0, UNITS)
            with sp.Fori(0, LOOPS) as i:
                for r in range(R):
                    step(i, r)
            step(LOOPS, 0, prep=False)

            sp.dma_start(gw[:, :, :], gate_w.rearrange("(c p) e -> p c e", p=P)).then_inc(gate_in, 16)
            sp.dma_start(gb[:, :], gate_b.rearrange("(o e) -> o e", o=1).broadcast_to([P, E])).then_inc(gate_in, 16)
            for e in range(2):
                sp.dma_start(W[:, e], expert_w[e].rearrange("(c p) n -> p c n", p=P)).then_inc(w_in[e], 16)
            sp.wait_ge(out_done, OUT_CREDIT + N)
            for e in range(E):
                sp.dma_start(eb[:, e, :], expert_b[e:e + 1, :].broadcast_to([P, D])).then_inc(bias_in, 16)
            for e in range(2, E):
                sp.wait_ge(y_full, T * (e - 1))
                sp.dma_start(W[:, e % 2], expert_w[e].rearrange("(c p) n -> p c n", p=P)).then_inc(w_in[e % 2], 16)
            for t in range(T):
                sp.wait_ge(acc_done, (E - 1) * T + t + 1)
                sp.dma_start(out_tiles[:, t], x1[:, t]).then_inc(stored, 16)
            sp.wait_ge(stored, 16 * T)

        @block.gpsimd
        def _(pool):
            pool.memset(ident[:, :], 0.0).then_inc(const0, 1)
            pool.memset(mask_qk[:, :], 0.0).then_inc(const0, 1)
            pool.memset(mask_kq[:, :], 0.0).then_inc(const0, 1)
            pool.memset(ones[:, :], 1.0).then_inc(const0, 1)
            pool.memset(eps[:, :], EPS).then_inc(const0, 1)
            pool.memset(mx[:, :], 0.0).then_inc(const0, 1)
            pool.memset(identb[:, :], 0.0).then_inc(const0, 1)
            pool.wait_ge(const0, 7)
            pool.affine_select(out=ident[:, :], in_=ident[:, :], compare_op=ALU.not_equal, fill=1.0,
                               base=0, pattern=[[-1, P]], channel_multiplier=1).then_inc(const0, 1)
            pool.affine_select(out=mask_qk[:, :], in_=mask_qk[:, :], compare_op=ALU.is_ge, fill=NEG,
                               base=0, pattern=[[-1, P]], channel_multiplier=1).then_inc(const, 1)
            pool.affine_select(out=mask_kq[:, :], in_=mask_kq[:, :], compare_op=ALU.is_ge, fill=NEG,
                               base=0, pattern=[[1, P]], channel_multiplier=-1).then_inc(const, 1)
            pool.affine_select(out=identb[:, :], in_=identb[:, :], compare_op=ALU.not_equal, fill=1.0,
                               base=0, pattern=[[-1, P]], channel_multiplier=1).then_inc(const, 1)
            pool.iota(iota[:, :], pattern=[[1, E]], base=0, channel_multiplier=0,
                      allow_small_or_imprecise_dtypes=True).then_inc(const, 1)

            def split(i, r):
                n = R * i + r
                b = n // NG
                first = isinstance(n, int) and n == 0
                ip, rp = at(i, r, R - 1)
                if not first:
                    pool.wait_ge(kst_in[rp], 16 * COPIES * ip)
                pool.wait_ge(split_done, SPLITS * n + 1)
                pool.tensor_tensor(k_lo[:, :], k_raw[:, r], k_hi[:, :].bitcast(F32), ALU.subtract).then_inc(split_done, 1)
                pool.wait_ge(xraw_in[r], 16 * (i + 1))
                pool.wait_ge(row_done, 2 * B if not isinstance(n, int) else 2 * (b + 1))
                row = [m[:, bass.ds(b * QT, QT), :].rearrange("p t q -> p (t q)") for m in (rstd_row, nmr_row)]
                pool.tensor_tensor(qn[:, :], x_raw[:, r], row[0], ALU.mult).then_inc(split_done, 1)
                pool.wait_ge(split_done, SPLITS * n + 3)
                pool.tensor_tensor(qn[:, :], qn[:, :], row[1], ALU.add).then_inc(split_done, 1)
                if not first:
                    pool.wait_ge(qst_in[rp], 16 * COPIES * ip)
                pool.wait_ge(split_done, SPLITS * n + 5)
                pool.tensor_tensor(q_lo[:, :], qn[:, :], q_hi[:, :].bitcast(F32), ALU.subtract).then_inc(split_done, 1)

            split(0, 0)
            split(0, 1)
            with pool.Fori(0, LOOPS) as i:
                for r in range(R):
                    split(*at(i, r, 2))

            def add_expert(e):
                for t in range(T):
                    pool.wait_ge(relu_done, T * e + t + 1)
                    if not isinstance(e, int) or e:
                        pool.wait_ge(acc_done, T * (e - 1) + t + 1)
                    pool.tensor_tensor(x1[:, t], x1[:, t], relu[:, t % 2], ALU.add).then_inc(acc_done, 1)

            add_expert(0)
            with pool.Fori(1, E) as e:
                add_expert(e)

        @block.scalar
        def _(act):
            act.wait_ge(const0, 7)
            for b in range(B):
                ts = slice(b * QT, (b + 1) * QT)
                act.wait_ge(stat_done, b * (2 * QT + 2) + 2 * QT)
                nc.scalar.activation(std[:, ts], mv[:, ts, 1], ACT.Sqrt, bias=eps[:, :]).then_inc(std_done, 1)
            def rows(b):
                act.wait_ge(row_full, 2 * QT * (b + 1))
                for which, row in enumerate((rstd_row, nmr_row)):
                    nc.scalar.copy(row[:, b * QT:(b + 1) * QT].rearrange("p t q -> p (t q)"),
                                   banks[ROW_BANK[b][which]]).then_inc(row_done, 1)

            def keys_high(i, r):
                n = R * i + r
                act.wait_ge(kraw_in[r], 16 * (i + 1))
                if not (isinstance(n, int) and n == 0):
                    ip, rp = at(i, r, R - 1)
                    act.wait_ge(kst_in[rp], 16 * COPIES * ip)
                    act.wait_ge(split_done, SPLITS * n)
                nc.scalar.copy(k_hi[:, :], k_raw[:, r]).then_inc(split_done, 1)

            def queries_high(i, r):
                n = R * i + r
                if not (isinstance(n, int) and n == 0):
                    ip, rp = at(i, r, R - 1)
                    act.wait_ge(qst_in[rp], 16 * COPIES * ip)
                act.wait_ge(split_done, SPLITS * n + 4)
                nc.scalar.copy(q_hi[:, :], qn[:, :]).then_inc(split_done, 1)

            def load_group(n, r):
                act.wait_ge(split_done, SPLITS * (n - 1))
                act.dma_start(k_raw[:, r:r + 1], ctx_T[bass.ds(n, 1)].rearrange("o p s -> p o s")).then_inc(kraw_in[r], 16)
                act.dma_start(x_raw[:, r:r + 1], x_T[bass.ds(n, 1)].rearrange("o p s -> p o s")).then_inc(xraw_in[r], 16)

            def load_values(n, r):
                act.wait_ge(pv_done, PV_CREDIT + KT * (n - 1))
                act.dma_start(val[:, r], ctx[bass.ds(n, 1)].rearrange("o (c p) d -> p (o c) d", p=P)).then_inc(val_in[r], 16)

            def step(i, r, prep=True, following=True):
                n = R * i + r
                if prep:
                    load_group(n + 2, (r + 2) % R)
                for k, c in enumerate(ROUND):
                    if k == 2 and following:
                        load_values(n + 1, (r + 1) % R)
                    if k == 3 and prep:
                        keys_high(*at(i, r, 2))
                    if k == 5 and prep:
                        queries_high(*at(i, r, 2))
                    rnd = KT * n + k
                    act.wait_ge(pv_done, rnd + 1)
                    for j in range(HG):
                        act.wait_ge(sc_full, HG * rnd + j + 1)
                        q0 = q_from(c)
                        nc.scalar.activation(prob[:, k % NP, j, q0:], sc[j % 2][:, q0:], ACT.Exp,
                                             scale=SCALE).then_inc(exp_done, 1)

            keys_high(0, 0)
            rows(0)
            queries_high(0, 0)
            rows(1)
            keys_high(0, 1)
            queries_high(0, 1)
            with act.Fori(0, LOOPS) as i:
                for r in range(R):
                    step(i, r)
            step(LOOPS, 0, prep=False)
            step(LOOPS, 1, prep=False, following=False)

            act.wait_ge(post, 3 * T)
            nc.scalar.activation(std[:, :], mv[:, :, 1], ACT.Sqrt, bias=eps[:, :]).then_inc(norm2_done, 1)
            act.wait_ge(post, 3 * T + 2)
            for t in range(T):
                nc.scalar.activation(xn2[:, t], x1[:, t], ACT.Identity, bias=nmr[:, t:t + 1],
                                     scale=rstd[:, t:t + 1]).then_inc(norm2_done, 1)

            def weigh(e, t, first=False):
                act.wait_ge(hid_done, T * e + t + 1)
                if not (first and t < 2):
                    act.wait_ge(acc_done, T * e + t - 1)
                nc.scalar.activation(relu[:, t % 2], hid[:, t % 2], ACT.Relu,
                                     scale=wsel[:, t, bass.ds(e, 1)]).then_inc(relu_done, 1)

            for t in range(T):
                weigh(0, t, first=True)
            with act.Fori(1, E) as e:
                for t in range(T):
                    weigh(e, t)

        @block.vector
        def _(dve):
            for n, (counted, free) in enumerate(((exp_done, SC_CREDIT), (pv_done, PV_CREDIT), (out_done, OUT_CREDIT))):
                dve.memset(diag[:, 0, n:n + 1], 0.0).then_inc(counted, free)
            for b in range(B):
                for t in range(b * QT, (b + 1) * QT):
                    dve.wait_ge(x_in[t], 16)
                    dve.bn_stats(stats[:, t, :], x1[:, t]).then_inc(stat_done, 1)
                    dve.wait_ge(stat_done, b * (2 * QT + 2) + 2 * (t - b * QT) + 1)
                    dve.bn_aggr(mv[:, t, :], stats[:, t, :]).then_inc(stat_done, 1)
                ts = slice(b * QT, (b + 1) * QT)
                dve.wait_ge(std_done, b + 1)
                dve.reciprocal(rstd[:, ts], std[:, ts]).then_inc(stat_done, 1)
                dve.wait_ge(stat_done, b * (2 * QT + 2) + 2 * QT + 1)
                dve.scalar_tensor_tensor(out=nmr[:, ts], in0=mv[:, ts, 0], scalar=-1.0, in1=rstd[:, ts],
                                         op0=ALU.mult, op1=ALU.mult).then_inc(stat_done, 1)
                dve.wait_ge(stat_done, (b + 1) * (2 * QT + 2))
                for t in range(b * QT, (b + 1) * QT):
                    for which, col in enumerate((rstd, nmr)):
                        use = 2 * t + which
                        if use == 0:
                            dve.wait_ge(const0, 8)
                            for counted, free in ((exp_done, SC_CREDIT), (pv_done, PV_CREDIT), (out_done, OUT_CREDIT)):
                                dve.wait_ge(counted, free)
                        if use >= 2:
                            dve.wait_ge(row_full, use - 1)
                        dve.tensor_scalar(diag[:, which], ident[:, :], col[:, t:t + 1], None, ALU.mult)\
                           .then_inc(diag_done, 1)

            def unit(i, r, place, pos, kind, which):
                dve.wait_ge(ring_full, place + 1)
                full = ring[slot(pos)]
                if kind == "max":
                    seen = (KT - QT + 1 + which % QT) * P
                    dve.tensor_reduce(mx[:, which:which + 1], full[:, 0:seen], AX.X, ALU.max)\
                       .then_inc(ring_free, 1)
                else:
                    if not (isinstance(i, int) and i < 0):
                        dve.wait_ge(max_in[r], 16 * (i + 1))
                    dve.tensor_scalar(mrow[:, :], full[0:MAXU, 0:P], -1.0, None, ALU.mult)\
                       .then_inc(ring_free, 2)

            def units(i, r, a, b):
                flat = [u for rnd in plan() for u in rnd]
                for pos, kind, which in flat[a:b]:
                    unit(i, r, first_unit(i, r) + pos, pos, kind, which)

            def take_out(n):
                dve.wait_ge(pv_done, PV_CREDIT + KT * (n + 1))
                dve.reciprocal(rden[:, :], den[:, :]).then_inc(rec_done, 1)
                dve.wait_ge(rec_done, 1 + n)
                dve.tensor_tensor(attnT[:, bass.ds(n, 1), :].rearrange("p o q -> p (o q)"), num[:, :], rden[:, :],
                                  ALU.mult).then_inc(out_done, 1)

            EARLY = 2
            dve.wait_ge(const0, 7)
            units(-1, 2, 0, UNITS)
            units(0, 0, 0, EARLY)
            with dve.Fori(0, LOOPS) as i:
                for r in range(R):
                    units(i, r, EARLY, UNITS)
                    units(*at(i, r, 1), 0, EARLY)
                    take_out(R * i + r)
            units(LOOPS, 0, EARLY, UNITS)
            take_out(R * LOOPS)
            take_out(R * LOOPS + 1)

            done = [0]

            def post_step(instruction):
                done[0] += 1
                instruction.then_inc(post, 1)

            for t in range(T):
                dve.wait_ge(back_full, t + 1)
                post_step(dve.tensor_tensor(x1[:, t], banks[t % 2], x1[:, t], ALU.add))
                dve.wait_ge(post, done[0])
                post_step(dve.bn_stats(stats[:, t, :], x1[:, t]))
                dve.wait_ge(post, done[0])
                post_step(dve.bn_aggr(mv[:, t, :], stats[:, t, :]))
            dve.wait_ge(norm2_done, 1)
            post_step(dve.reciprocal(rstd[:, :], std[:, :]))
            dve.wait_ge(post, done[0])
            post_step(dve.scalar_tensor_tensor(out=nmr[:, :], in0=mv[:, :, 0], scalar=-1.0, in1=rstd[:, :],
                                               op0=ALU.mult, op1=ALU.mult))
            for t in range(T):
                dve.wait_ge(turn_full, t + 1)
                dve.tensor_copy(xT[:, t].rearrange("p c q -> p (c q)"), banks[2 + t % 2]).then_inc(turn_done, 1)
            dve.wait_ge(gate_full, 1)
            dve.wait_ge(gate_in, 32)
            for t in range(T):
                post_step(dve.tensor_tensor(logit[:, t, :], banks[4][:, t * E:(t + 1) * E], gb[:, :], ALU.add))
            dve.wait_ge(post, done[0])
            for t in range(T):
                post_step(dve.max(top[:, t, :], logit[:, t, :]))
            dve.wait_ge(post, done[0])
            for t in range(T):
                post_step(dve.max_index(topi[:, t, :], top[:, t, :], logit[:, t, :]))
            dve.wait_ge(post, done[0])
            post_step(dve.tensor_copy(topf[:, :, :], topi[:, :, :]))
            dve.wait_ge(post, done[0])
            dve.wait_ge(const, 4)
            for t in range(T):
                post_step(dve.tensor_scalar(hot[:, t, :], iota[:, :], topf[:, t, 0:1], 0.5, ALU.is_equal, ALU.mult))
                post_step(dve.tensor_scalar(hot2[:, t, :], iota[:, :], topf[:, t, 1:2], 0.5, ALU.is_equal, ALU.mult))
            dve.wait_ge(post, done[0])
            post_step(dve.tensor_tensor(wsel[:, :, :], hot[:, :, :], hot2[:, :, :], ALU.add))
            dve.wait_ge(post, done[0])

            dve.wait_ge(bias_in, 16 * E)

            def add_bias(e, t, first=False):
                dve.wait_ge(y_full, T * e + t + 1)
                if not (first and t < 2):
                    dve.wait_ge(relu_done, T * e + t - 1)
                dve.tensor_tensor(hid[:, t % 2], banks[t], eb[:, bass.ds(e, 1), :].rearrange("p o n -> p (o n)"),
                                  ALU.add).then_inc(hid_done, 1)

            for t in range(T):
                add_bias(0, t, first=True)
            with dve.Fori(1, E) as e:
                for t in range(T):
                    add_bias(e, t)

        @block.tensor
        def _(pe):
            pe.wait_ge(const, 3)
            pe.wait_ge(const0, 8)

            for use in range(2 * T):
                t, which = use // 2, use % 2
                pe.wait_ge(diag_done, use + 1)
                pe.matmul(banks[ROW_BANK[t // QT][which]][:, (t % QT) * P:(t % QT + 1) * P], ones[:, :],
                          diag[:, which], start=True, stop=True).then_inc(row_full, 1)
            pe.wait_ge(row_done, 2 * B)

            def unit(i, r, pos, kind, which):
                place = first_unit(i, r) + pos
                to = ring[slot(pos)]
                if kind == "turn":
                    pe.wait_ge(ring_free, place)
                    pe.transpose(to[:, 0:P], mx[:, :], ident[:, :]).then_inc(ring_full, 2)
                    return
                if not (isinstance(place, int) and place < 2):
                    pe.wait_ge(ring_free, place - 1)
                i1, r1 = at(i, r, 1)
                if which == 0:
                    pe.wait_ge(kst_in[r1], 16 * COPIES * (i1 + 1))
                    pe.wait_ge(qst_in[r1], 16 * COPIES * (i1 + 1))
                j, t = which // QT, which % QT
                q = qst[0:ROWS, r1, j, t * P:(t + 1) * P]
                seen = (KT - QT + 1 + t) * P
                pe.matmul(to[:, 0:512], q, kst[0:ROWS, r1, j, 0:512], start=True, stop=True)
                pe.matmul(to[:, 512:seen], q, kst[0:ROWS, r1, j, 512:seen], start=True, stop=False)
                pe.matmul(to[:, seen - P:seen], identb[:, :], mask_qk[:, :], start=False, stop=True)\
                  .then_inc(ring_full, 1)

            def score(i, r, k, j):
                n = R * i + r
                c = ROUND[k]
                place = HG * (KT * n + k) + j
                pe.wait_ge(exp_done, place + 1)
                if k == 0 and j == 0:
                    pe.wait_ge(max_in[r], 16 * (i + 1))
                q0 = q_from(c)
                masked = c >= KT - QT
                last = pe.matmul(sc[j % 2][:, q0:], kst[0:ROWS + 1, r, j, c * P:(c + 1) * P],
                                 qst[0:ROWS + 1, r, j, q0:], start=True, stop=not masked)
                if masked:
                    last = pe.matmul(sc[j % 2][:, q0:q0 + P], identb[:, :], mask_kq[:, :], start=False, stop=True)
                last.then_inc(sc_full, 1)

            def add_round(i, r, k):
                n = R * i + r
                c = ROUND[k]
                q0 = q_from(c)
                pe.wait_ge(exp_done, SC_CREDIT + HG * (KT * n + k + 1))
                if k == 0:
                    pe.wait_ge(val_in[r], 16 * (i + 1))
                    pe.wait_ge(out_done, OUT_CREDIT + n)
                for to, w in ((num, None), (den, ones)):
                    for j in range(HG):
                        heads = slice(j * HD, (j + 1) * HD)
                        left = val[:, r, c, heads] if w is None else ones[:, 0:HD]
                        last = pe.matmul(to[heads, q0:], left, prob[:, k % NP, j, q0:],
                                         start=(k == 0), stop=(k == KT - 1), tile_position=(0, j * HD))
                last.then_inc(pv_done, 1)

            def step(i, r, scores=True, maxima=True, following=True):
                for k in range(KT):
                    todo = plan()[k] if maxima else []
                    nxt = (i, r, k + 1) if k + 1 < KT else (*at(i, r, 1), 0) if following else None
                    for j in range(HG):
                        if scores and nxt:
                            score(*nxt, j)
                        for u in todo[j:j + 1]:
                            unit(i, r, *u)
                    if scores:
                        add_round(i, r, k)

            step(-1, 2, scores=False)
            pe.wait_ge(one_in, 16 * R)
            for j in range(HG):
                score(0, 0, 0, j)
            with pe.Fori(0, LOOPS) as i:
                for r in range(R):
                    step(i, r)
            step(LOOPS, 0)
            step(LOOPS, 1, maxima=False, following=False)

            for t in range(T):
                if t == 0:
                    pe.wait_ge(out_done, OUT_CREDIT + N)
                if t >= 2:
                    pe.wait_ge(post, 3 * (t - 2) + 1)
                b, q = t // QT, t % QT
                for g in range(NG):
                    last = pe.transpose(banks[t % 2][:, g * P:(g + 1) * P],
                                        attnT[:, b * NG + g, q * P:(q + 1) * P], ident[:, :])
                last.then_inc(back_full, 1)
            for t in range(T):
                pe.wait_ge(norm2_done, t + 2)
                if t >= 2:
                    pe.wait_ge(turn_done, t - 1)
                for c in range(KC):
                    last = pe.transpose(banks[2 + t % 2][:, c * P:(c + 1) * P], xn2[:, t, c * P:(c + 1) * P],
                                        ident[:, :])
                last.then_inc(turn_full, 1)
            pe.wait_ge(gate_in, 32)
            for t in range(T):
                pe.wait_ge(turn_done, t + 1)
                for c in range(KC):
                    last = pe.matmul(banks[4][:, t * E:(t + 1) * E], xT[:, t, c, :], gw[:, c, :],
                                     start=(c == 0), stop=(c == KC - 1))
            last.then_inc(gate_full, 1)

            def expert(i, e, first=False):
                pe.wait_ge(w_in[e], 16 * (i + 1))
                for t in range(T):
                    if not (first and e == 0):
                        pe.wait_ge(hid_done, T * (2 * i + e - 1) + t + 1)
                    for c in range(KC):
                        last = pe.matmul(banks[t], xT[:, t, c, :], W[:, e, c, :], start=(c == 0), stop=(c == KC - 1))
                    last.then_inc(y_full, 1)

            pe.wait_ge(post, 3 * T + 2 + T)
            expert(0, 0, first=True)
            expert(0, 1, first=True)
            with pe.Fori(1, E // 2) as i:
                for e in range(2):
                    expert(i, e)


_INS = ['x', 'x_T', 'ctx', 'ctx_T', 'L0_ffn_gate_w', 'L0_ffn_gate_b', 'L0_ffn_expert_w', 'L0_ffn_expert_b']
_OUTS = [((2, 512, 512), 'float32')]


def kernel(**inputs):
    import numpy as _np
    import concourse.bacc as _bacc
    from concourse import mybir as _mybir
    from concourse.bass_utils import run_bass_kernel_spmd as _run

    nc = _bacc.Bacc("TRN2", target_bir_lowering=False, num_devices=1)
    arrays, args = {}, []
    x, ctx = _np.asarray(inputs['x']), _np.asarray(inputs['ctx_2048'])
    b, sq, d = x.shape
    sk = ctx.shape[1]
    inputs['x_T'] = x.transpose(0, 2, 1).reshape(b * d // P, P, sq)
    inputs['ctx_T'] = ctx.transpose(0, 2, 1).reshape(b * d // P, P, sk)
    inputs['ctx'] = ctx.reshape(b, sk, d // P, P).transpose(0, 2, 1, 3).reshape(b * d // P, sk, P)
    for name in _INS:
        a = _np.ascontiguousarray(inputs[name])
        arrays[f"in_{name}_dram"] = a
        args.append(nc.dram_tensor(f"in_{name}_dram", a.shape, _mybir.dt.from_np(a.dtype), kind="ExternalInput").ap())
    for i, (shape, dtype) in enumerate(_OUTS):
        dt = _mybir.dt.from_np(_np.dtype(dtype))
        args.append(nc.dram_tensor(f"out_{i}_dram", shape, dt, kind="ExternalOutput").ap())
    bass_cross_attention_moe(nc, *args)
    r = _run(nc, [arrays], core_ids=[0])
    got = tuple(r.results[0][f"out_{i}_dram"] for i in range(len(_OUTS)))
    return got[0]
```

```python
import concourse.bass as bass
from concourse import mybir
from contextlib import ExitStack

F32 = mybir.dt.float32
F32R = mybir.dt.float32r
BF16 = mybir.dt.bfloat16
U32 = mybir.dt.uint32
I32 = mybir.dt.int32
ALU = mybir.AluOpType
ACT = mybir.ActivationFunctionType
AX = mybir.AxisListType

P = 128
HEADS = 16
NEG = -1e30
EPS = 1e-5


def bass_cross_attention_moe(nc, x, x_T, ctx, ctx_T, gate_w, gate_b, expert_w, expert_b, out,
                              xn_rows, y_rows):
    B, SQ, D = x.shape
    SK = ctx.shape[1]
    E = gate_w.shape[1]
    HD = D // HEADS
    HG = P // HD
    NG = D // P
    N = B * NG
    QT = SQ // P
    KT = SK // P
    T = B * QT
    KC = D // P
    SCALE = float(HD) ** -0.5
    ROWS = 3 * HD
    R = 3
    NP = 2
    SPLITS = 6
    MAXU = HG * QT
    UNITS = MAXU + 2
    COPIES = 3 * HG
    ROUND = [0] + list(range(KT - QT + 1, KT)) + list(range(1, KT - QT + 1))
    AHEAD = 4
    PLAN = [3, 2, 1, 1, 3, 2, 3, 2]
    LOOPS = (N - 2) // R
    C = 2 * T
    G = C + E - 1
    U = 4
    assert HD == 32 and HG == 4 and SQ == 512 and SK == 1024 and (N - 2) % R == 0 and UNITS % 2 == 0

    def q_from(c):
        return max(0, c - (KT - QT)) * P

    def at(i, r, k):
        return i + (r + k) // R, (r + k) % R

    def place(n, which):
        return UNITS * n + which

    def plan(prologue=False, following=True):
        units = [(1, w) for w in range(0 if prologue else AHEAD, MAXU + 1)]
        if following:
            units += [(2, w) for w in range(AHEAD)]
        rounds, k = [], 0
        for c in PLAN:
            rounds.append(units[k:k + c])
            k += c
        rounds[-1] += units[k:]
        return rounds

    outer = ExitStack()
    with outer:
        def tensor(stack, name, shape, dt=F32):
            return stack.enter_context(nc.sbuf_tensor(name, shape, dt))

        def sem(name):
            return outer.enter_context(nc.semaphore(name))

        def sems(name):
            return [sem(f"{name}{r}") for r in range(R)]

        ident = tensor(outer, "ident", [P, P])
        identb = tensor(outer, "identb", [P, P], BF16)
        mask_qk = tensor(outer, "mask_qk", [P, P], BF16)
        mask_kq = tensor(outer, "mask_kq", [P, P], BF16)
        ones = tensor(outer, "ones", [P, P])
        stats = tensor(outer, "stats", [P, T, 6])
        mv = tensor(outer, "mv", [P, T, 2])
        std = tensor(outer, "std", [P, T])
        rstd = tensor(outer, "rstd", [P, T])
        nmr = tensor(outer, "nmr", [P, T])
        eps = tensor(outer, "eps", [P, 1])
        x1 = tensor(outer, "x1", [P, T, D])
        gw = tensor(outer, "gw", [P, KC, E])
        gb = tensor(outer, "gb", [P, E])
        iota = tensor(outer, "iota", [P, E])

        inner = ExitStack()
        attnT = tensor(inner, "attnT", [P, N, SQ])
        denT = tensor(inner, "denT", [P, N, SQ])
        rstd_row = tensor(inner, "rstd_row", [P, T, P])
        nmr_row = tensor(inner, "nmr_row", [P, T, P])
        diag = tensor(inner, "diag", [P, 2, P])
        k_raw = tensor(inner, "k_raw", [P, SK])
        x_raw = tensor(inner, "x_raw", [P, SQ])
        val = tensor(inner, "val", [P, R, KT, P])
        k_hi = tensor(inner, "k_hi", [P, SK], F32R)
        k_lo = tensor(inner, "k_lo", [P, SK], F32R)
        qn = tensor(inner, "qn", [P, SQ])
        q_hi = tensor(inner, "q_hi", [P, SQ], F32R)
        q_lo = tensor(inner, "q_lo", [P, SQ], F32R)
        kst = tensor(inner, "kst", [P, R, HG, SK], F32R)
        qst = tensor(inner, "qst", [P, R, HG, SQ], F32R)
        mx = tensor(inner, "mx", [P, P])
        zeros = tensor(inner, "zeros", [MAXU, P])
        mrow = tensor(inner, "mrow", [MAXU, P], F32R)
        prob = tensor(inner, "prob", [P, NP, HG, SQ])
        blank = prob[:, :, :, :].rearrange("p b j q -> p (b j q)")
        inner.close()

        late = ExitStack()
        w_hi = tensor(late, "w_hi", [P, E, KC, D], F32R)
        w_lo = tensor(late, "w_lo", [P, E, KC, D], F32R)
        eb = tensor(late, "eb", [P, E, D])
        logit = tensor(late, "logit", [P, T, E])
        top = tensor(late, "top", [P, T, 8])
        topi = tensor(late, "topi", [P, T, 8], U32)
        topf = tensor(late, "topf", [P, T, 8])
        rden = tensor(late, "rden", [P, T, HEADS])
        pick = tensor(late, "pick", [P, T, 2, E])
        both = tensor(late, "both", [P, T, E], BF16)
        where = tensor(late, "where", [P, T, E])
        prod = tensor(late, "prod", [P, T, 2, E])
        tiles_cmp = tensor(late, "tiles_cmp", [P, E, T])
        tiles = tensor(late, "tiles", [P, E])
        before_cmp = tensor(late, "before_cmp", [P, E, E])
        base_cmp = tensor(late, "base_cmp", [P, E, E])
        base = tensor(late, "base", [P, E])
        base_slot = tensor(late, "base_slot", [P, E])
        end = tensor(late, "end", [P, E])
        owner_cmp = tensor(late, "owner_cmp", [P, G, E])
        owner = tensor(late, "owner", [P, G])
        owner_id = tensor(late, "owner_id", [P, G], I32)
        pos = tensor(late, "pos", [P, C])
        pos_cmp = tensor(late, "pos_cmp", [P, C, G])
        pos_tile = tensor(late, "pos_tile", [P, C])
        pos_lane = tensor(late, "pos_lane", [P, C])
        tile_hot = tensor(late, "tile_hot", [P, C, G])
        tile_id = tensor(late, "tile_id", [P, C, G])
        dump = tensor(late, "dump", [P, G])
        back = tensor(late, "back", [P, G])
        flat = tensor(late, "flat", [P, G])
        y_row = tensor(late, "y_row", [P, G], I32)
        x_row = tensor(late, "x_row", [P, G], I32)
        count_step = tensor(late, "count_step", [P, T])
        tile_step = tensor(late, "tile_step", [P, G])
        tile_next = tensor(late, "tile_next", [P, G])
        lane = tensor(late, "lane", [P, P])
        choice_id = tensor(late, "choice_id", [P, C])
        spare_row = tensor(late, "spare_row", [P, 1])
        upper = tensor(late, "upper", [P, P], BF16)
        ones_b = tensor(late, "ones_b", [P, P], BF16)
        gating = ExitStack()
        xn2 = tensor(gating, "xn2", [P, T, D])
        xT = tensor(gating, "xT", [P, 2, KC, P])
        att = tensor(gating, "att", [P, 2, D])
        gating.close()
        slots = ExitStack()
        lane_hot = tensor(slots, "lane_hot", [P, C, P])
        slots.close()
        turning = ExitStack()
        x_hi = tensor(turning, "x_hi", [P, 2, KC, P], F32R)
        x_lo = tensor(turning, "x_lo", [P, 2, KC, P], F32R)
        xg = tensor(turning, "xg", [P, U, D])
        hid = tensor(turning, "hid", [P, 2, D])
        y = tensor(turning, "y", [P, U, D])
        turning.close()
        late.close()

        final = ExitStack()
        chosen = tensor(final, "chosen", [P, T, 2, D])
        final.close()

        ring = [outer.enter_context(nc.psum_tensor(f"ring{s}", [P, 2 * 512], F32)) for s in range(2)]
        sc = [outer.enter_context(nc.psum_tensor(f"sc{s}", [P, 512], F32)) for s in range(2)]
        num = outer.enter_context(nc.psum_tensor("num", [P, 512], F32))
        den = outer.enter_context(nc.psum_tensor("den", [P, 512], F32))
        banks = [ring[0][:, 0:512], ring[0][:, 512:1024], ring[1][:, 0:512], ring[1][:, 512:1024],
                 sc[0][:, :], sc[1][:, :], num[:, :], den[:, :]]

        ROW_BANK = ((6, 7), (4, 5))

        choice_step, hot_step, owner_step = [], [], []
        BACK = 5

        SC_CREDIT, PV_CREDIT, OUT_CREDIT = 2, NP, 1
        const0 = sem("const0")
        const = sem("const")
        one_in = sem("one_in")
        x_in = [sem(f"x_in{t}") for t in range(T)]
        stat_done = sem("stat_done")
        std_done = sem("std_done")
        diag_done = sem("diag_done")
        row_full = sem("row_full")
        row_done = sem("row_done")
        kraw_in, xraw_in = sem("kraw_in"), sem("xraw_in")
        val_in = sems("val_in")
        split_done = sem("split_done")
        kst_in, qst_in = sem("kst_in"), sem("qst_in")
        max_in = sem("max_in")
        ring_full = sem("ring_full")
        ring_free = sem("ring_free")
        sc_full = sem("sc_full")
        exp_done = sem("exp_done")
        pv_done = sem("pv_done")
        den_done = sem("den_done")
        out_done = sem("out_done")
        gate_in = sem("gate_in")
        bias_in = sem("bias_in")
        back_full = sem("back_full")
        post = sem("post")
        norm2_done = sem("norm2_done")
        turn_full = sem("turn_full")
        turn_done = sem("turn_done")
        gate_full = sem("gate_full")
        w_in = [sem(f"w_in{e}") for e in range(E)]
        w_high = sem("w_high")
        w_low = sem("w_low")
        slot_const = sem("slot_const")
        xn_out = sem("xn_out")
        rank_full = sem("rank_full")
        ids_full = sem("ids_full")
        rows_done = sem("rows_done")
        xg_in = [sem(f"xg_in{r}") for r in range(U)]
        tr_full = sem("tr_full")
        high_done = sem("high_done")
        low_done = sem("low_done")
        y_full = sem("y_full")
        hid_done = sem("hid_done")
        relu_done = sem("relu_done")
        y_out = sem("y_out")
        chosen_in = [sem(f"chosen_in{t}") for t in range(T)]
        sum_done = [sem("sum_dve"), sem("sum_pool")]
        stored = sem("stored")

        x_tiles = x.rearrange("b (t p) d -> p (b t) d", p=P)
        out_tiles = out.rearrange("b (t p) d -> p (b t) d", p=P)

        xn_tiles = xn_rows.rearrange("(t p) d -> p t d", p=P)
        y_tiles = y_rows[0:C * P].rearrange("(j t p) d -> p t j d", j=2, p=P)

        block = outer.enter_context(nc.Block())

        @block.sync
        def _(sp):
            def stack(r, n):
                if isinstance(n, int) and n < 2:
                    sp.wait_ge(split_done, SPLITS * n + 2)
                else:
                    sp.wait_ge(exp_done, SC_CREDIT + HG * KT * (n - 2) + 1)
                for to, half in ((0, k_hi), (1, k_hi), (2, k_lo)):
                    for j in range(HG):
                        sp.dma_start(kst[to * HD:(to + 1) * HD, r, j, :].bitcast(F32),
                                     half[j * HD:(j + 1) * HD, :].bitcast(F32)).then_inc(kst_in, 16)
                sp.wait_ge(split_done, SPLITS * (n + 1))
                for to, half in ((0, q_hi), (1, q_lo), (2, q_hi)):
                    for j in range(HG):
                        sp.dma_start(qst[to * HD:(to + 1) * HD, r, j, :].bitcast(F32),
                                     half[j * HD:(j + 1) * HD, :].bitcast(F32)).then_inc(qst_in, 16)
                sp.dma_start(qst[ROWS:ROWS + 1, r].bitcast(F32).rearrange("o j (t q) -> o (j t) q", q=P),
                             zeros[:, :]).then_inc(qst_in, 16)

            def send_max(r, taken):
                sp.wait_ge(ring_free, taken)
                sp.dma_start(qst[ROWS:ROWS + 1, r].bitcast(F32).rearrange("o j (t q) -> o (j t) q", q=P),
                             mrow[:, :].bitcast(F32)).then_inc(max_in, 16)

            def load_values(r, n):
                sp.dma_start(val[:, r], ctx[bass.ds(n, 1)].rearrange("o (c p) d -> p (o c) d", p=P)).then_inc(val_in[r], 16)

            def step(i, r, prep=True):
                n = R * i + r
                load_values((r + 1) % R, n + 1)
                if prep:
                    stack((r + 2) % R, n + 2)
                send_max((r + 1) % R, UNITS * (n + 2))

            sp.dma_start(k_raw[:, :], ctx_T[0]).then_inc(kraw_in, 16)
            for t in range(T):
                sp.dma_start(x1[:, t], x_tiles[:, t]).then_inc(x_in[t], 16)
                if t == QT - 1:
                    sp.dma_start(x_raw[:, :], x_T[0]).then_inc(xraw_in, 16)
            sp.wait_ge(const0, 9)
            for r in range(R):
                sp.dma_start(kst[ROWS:ROWS + 1, r].bitcast(F32).rearrange("o j (t k) -> o (j t) k", k=P),
                             ones[0:HG * KT, :]).then_inc(one_in, 16)
                sp.dma_start(kst[ROWS + 1:P, r].bitcast(F32).rearrange("p j s -> p (j s)"),
                             blank[0:P - ROWS - 1, :]).then_inc(one_in, 16)
                sp.dma_start(qst[ROWS + 1:P, r].bitcast(F32).rearrange("p j s -> p (j s)"),
                             blank[0:P - ROWS - 1, 0:HG * SQ]).then_inc(one_in, 16)
            stack(0, 0)
            load_values(0, 0)
            stack(1, 1)
            send_max(0, UNITS)
            with sp.Fori(0, LOOPS) as i:
                for r in range(R):
                    step(i, r)
            step(LOOPS, 0, prep=False)

            sp.dma_start(gw[:, :, :], gate_w.rearrange("(c p) e -> p c e", p=P)).then_inc(gate_in, 16)
            sp.dma_start(gb[:, :], gate_b.rearrange("(o e) -> o e", o=1).broadcast_to([P, E])).then_inc(gate_in, 16)
            sp.wait_ge(out_done, OUT_CREDIT + N)
            for e in range(E):
                if e == E // 2:
                    for o in range(E):
                        sp.dma_start(eb[:, o, :], expert_b[o:o + 1, :].broadcast_to([P, D])).then_inc(bias_in, 16)
                sp.dma_start(w_lo[:, e].bitcast(F32), expert_w[e].rearrange("(c p) n -> p c n", p=P))\
                  .then_inc(w_in[e], 16)
            for t in range(T):
                sp.wait_ge(norm2_done, t + 2)
                sp.dma_start(xn_tiles[:, t], xn2[:, t]).then_inc(xn_out, 16)
            sp.wait_ge(y_out, 16 * G)
            for t in range(T):
                sp.dma_start(chosen[:, t], y_tiles[:, t]).then_inc(chosen_in[t], 16)
            for t in range(T):
                sp.wait_ge(sum_done[t % 2], 2 * (t // 2 + 1))
                sp.dma_start(out_tiles[:, t], x1[:, t]).then_inc(stored, 16)
            sp.wait_ge(stored, 16 * T)
            sp.wait_ge(xn_out, 16 * T)

        @block.gpsimd
        def _(pool):
            pool.memset(ident[:, :], 0.0).then_inc(const0, 1)
            pool.memset(mask_qk[:, :], 0.0).then_inc(const0, 1)
            pool.memset(mask_kq[:, :], 0.0).then_inc(const0, 1)
            pool.memset(ones[:, :], 1.0).then_inc(const0, 1)
            pool.memset(eps[:, :], EPS).then_inc(const0, 1)
            pool.memset(mx[:, :], 0.0).then_inc(const0, 1)
            pool.memset(identb[:, :], 0.0).then_inc(const0, 1)
            pool.memset(zeros[:, :], 0.0).then_inc(const0, 1)
            pool.memset(blank[:, :], 0.0).then_inc(const0, 1)
            pool.wait_ge(const0, 9)
            pool.affine_select(out=ident[:, :], in_=ident[:, :], compare_op=ALU.not_equal, fill=1.0,
                               base=0, pattern=[[-1, P]], channel_multiplier=1).then_inc(const0, 1)
            pool.affine_select(out=mask_qk[:, :], in_=mask_qk[:, :], compare_op=ALU.is_ge, fill=NEG,
                               base=0, pattern=[[-1, P]], channel_multiplier=1).then_inc(const, 1)
            pool.affine_select(out=mask_kq[:, :], in_=mask_kq[:, :], compare_op=ALU.is_ge, fill=NEG,
                               base=0, pattern=[[1, P]], channel_multiplier=-1).then_inc(const, 1)
            pool.affine_select(out=identb[:, :], in_=identb[:, :], compare_op=ALU.not_equal, fill=1.0,
                               base=0, pattern=[[-1, P]], channel_multiplier=1).then_inc(const, 1)
            pool.iota(iota[:, :], pattern=[[1, E]], base=0, channel_multiplier=0,
                      allow_small_or_imprecise_dtypes=True).then_inc(const, 1)

            def split(n):
                b = n // NG
                first = isinstance(n, int) and n == 0
                if not first:
                    pool.wait_ge(kst_in, 16 * COPIES * n)
                pool.wait_ge(split_done, SPLITS * n + 1)
                pool.tensor_tensor(k_lo[:, :], k_raw[:, :], k_hi[:, :].bitcast(F32), ALU.subtract).then_inc(split_done, 1)
                pool.wait_ge(xraw_in, 16 * (n + 1))
                pool.wait_ge(row_done, 2 * B if not isinstance(n, int) else 2 * (b + 1))
                row = [m[:, bass.ds(b * QT, QT), :].rearrange("p t q -> p (t q)") for m in (rstd_row, nmr_row)]
                pool.tensor_tensor(qn[:, :], x_raw[:, :], row[0], ALU.mult).then_inc(split_done, 1)
                pool.wait_ge(split_done, SPLITS * n + 3)
                pool.tensor_tensor(qn[:, :], qn[:, :], row[1], ALU.add).then_inc(split_done, 1)
                if not first:
                    pool.wait_ge(qst_in, 16 * (COPIES + 1) * n)
                pool.wait_ge(split_done, SPLITS * n + 5)
                pool.tensor_tensor(q_lo[:, :], qn[:, :], q_hi[:, :].bitcast(F32), ALU.subtract).then_inc(split_done, 1)

            for n in range(R):
                split(n)
            with pool.Fori(R, N) as n:
                split(n)

            pool.wait_ge(out_done, OUT_CREDIT + N)
            pool.wait_ge(den_done, OUT_CREDIT + N)
            pool.memset(ones_b[:, :], 1.0).then_inc(slot_const, 1)
            pool.memset(upper[:, :], 1.0).then_inc(slot_const, 1)
            pool.wait_ge(slot_const, 2)
            pool.affine_select(out=upper[:, :], in_=upper[:, :], compare_op=ALU.is_gt, fill=0.0,
                               base=0, pattern=[[1, P]], channel_multiplier=-1).then_inc(slot_const, 1)
            for to, pattern, first, by_partition in (
                    (count_step, [[P, T]], 0, 0), (tile_step, [[P, G]], 0, 0), (tile_next, [[1, G]], 1, 0),
                    (lane, [[1, P]], -P, 0), (choice_id, [[P, T], [B * SQ, 2]], 1, 1),
                    (spare_row, [[1, 1]], 2 * B * SQ + 1, 1)):
                pool.iota(to[:, :], pattern=pattern, base=first, channel_multiplier=by_partition,
                          allow_small_or_imprecise_dtypes=True).then_inc(slot_const, 1)

            for e in range(E):
                pool.wait_ge(w_high, e + 1)
                pool.tensor_tensor(w_lo[:, e].rearrange("p c n -> p (c n)"),
                                   w_lo[:, e].bitcast(F32).rearrange("p c n -> p (c n)"),
                                   w_hi[:, e].bitcast(F32).rearrange("p c n -> p (c n)"), ALU.subtract).then_inc(w_low, 1)

            def gather(g):
                if g >= U:
                    pool.wait_ge(tr_full, g - U + 1)
                pool.indirect_dma_start(xg[:, g % U], None, xn_rows[:, :],
                                        bass.IndirectOffsetOnAxis(ap=x_row[:, g:g + 1], axis=0)).then_inc(xg_in[g % U], 16)

            def scatter(g):
                if g:
                    pool.wait_ge(y_out, 16 * g)
                pool.wait_ge(relu_done, g + 1)
                pool.indirect_dma_start(y_rows[:, :], bass.IndirectOffsetOnAxis(ap=y_row[:, g:g + 1], axis=0),
                                        y[:, g % U], None).then_inc(y_out, 16)

            pool.wait_ge(rows_done, 2)
            pool.wait_ge(ids_full, 1)
            pool.wait_ge(xn_out, 16 * T)
            for g in range(U):
                gather(g)
            for g in range(G):
                if g + U < G:
                    gather(g + U)
                scatter(g)

            for t in range(1, T, 2):
                pool.wait_ge(chosen_in[t], 16)
                pool.tensor_tensor(x1[:, t], x1[:, t], chosen[:, t, 0], ALU.add).then_inc(sum_done[1], 1)
                pool.wait_ge(sum_done[1], t)
                pool.tensor_tensor(x1[:, t], x1[:, t], chosen[:, t, 1], ALU.add).then_inc(sum_done[1], 1)

        @block.scalar
        def _(act):
            act.wait_ge(const0, 9)
            for b in range(B):
                ts = slice(b * QT, (b + 1) * QT)
                act.wait_ge(stat_done, b * (2 * QT + 2) + 2 * QT)
                nc.scalar.activation(std[:, ts], mv[:, ts, 1], ACT.Sqrt, bias=eps[:, :]).then_inc(std_done, 1)
            def rows(b):
                act.wait_ge(row_full, 2 * QT * (b + 1))
                for which, row in enumerate((rstd_row, nmr_row)):
                    nc.scalar.copy(row[:, b * QT:(b + 1) * QT].rearrange("p t q -> p (t q)"),
                                   banks[ROW_BANK[b][which]]).then_inc(row_done, 1)

            def keys_high(n):
                act.wait_ge(kraw_in, 16 * (n + 1))
                if not (isinstance(n, int) and n == 0):
                    act.wait_ge(kst_in, 16 * COPIES * n)
                    act.wait_ge(split_done, SPLITS * n)
                nc.scalar.copy(k_hi[:, :], k_raw[:, :]).then_inc(split_done, 1)

            def queries_high(n):
                if not (isinstance(n, int) and n == 0):
                    act.wait_ge(qst_in, 16 * (COPIES + 1) * n)
                act.wait_ge(split_done, SPLITS * n + 4)
                nc.scalar.copy(q_hi[:, :], qn[:, :]).then_inc(split_done, 1)

            def load_group(n):
                act.wait_ge(split_done, SPLITS * n)
                act.dma_start(k_raw[:, :], ctx_T[bass.ds(n, 1)].rearrange("o p s -> p (o s)")).then_inc(kraw_in, 16)
                act.dma_start(x_raw[:, :], x_T[bass.ds(n, 1)].rearrange("o p s -> p (o s)")).then_inc(xraw_in, 16)

            def exps(n, k):
                q0 = q_from(ROUND[k])
                rnd = KT * n + k
                act.wait_ge(pv_done, rnd + 1)
                for j in range(HG):
                    act.wait_ge(sc_full, HG * rnd + j + 1)
                    nc.scalar.activation(prob[:, k % NP, j, q0:], sc[j % 2][:, q0:], ACT.Exp,
                                         scale=SCALE).then_inc(exp_done, 1)

            def take_sums(n):
                act.wait_ge(pv_done, PV_CREDIT + KT * (n + 1))
                nc.scalar.copy(denT[:, bass.ds(n, 1), :].rearrange("p o q -> p (o q)"), den[:, :]).then_inc(den_done, 1)

            def step(n, prep=True, following=True):
                if prep:
                    load_group(n + 3)
                for k in range(1, KT):
                    exps(n, k)
                    if k == 4 and prep:
                        keys_high(n + 3)
                    if k == 7 and prep:
                        queries_high(n + 3)
                if following:
                    exps(n + 1, 0)
                take_sums(n)

            keys_high(0)
            rows(0)
            queries_high(0)
            rows(1)
            for n in (1, 2):
                load_group(n)
                keys_high(n)
                queries_high(n)
            exps(0, 0)
            with act.Fori(0, N - R) as n:
                step(n)
            for n in range(N - R, N):
                step(n, prep=False, following=n + 1 < N)

            act.wait_ge(post, BACK * T)
            nc.scalar.activation(std[:, :], mv[:, :, 1], ACT.Sqrt, bias=eps[:, :]).then_inc(norm2_done, 1)
            act.wait_ge(post, BACK * T + 2)
            for t in range(T):
                nc.scalar.activation(xn2[:, t], x1[:, t], ACT.Identity, bias=nmr[:, t:t + 1],
                                     scale=rstd[:, t:t + 1]).then_inc(norm2_done, 1)

            act.wait_ge(back_full, T)
            for e in range(E):
                act.wait_ge(w_in[e], 16)
                nc.scalar.copy(w_hi[:, e].rearrange("p c n -> p (c n)"),
                               w_lo[:, e].bitcast(F32).rearrange("p c n -> p (c n)")).then_inc(w_high, 1)

            def turned_high(i, r, first=False):
                g = U * i + r
                act.wait_ge(tr_full, g + 1)
                if not (first and r < 2):
                    act.wait_ge(y_full, g - 1)
                nc.scalar.copy(x_hi[:, r % 2].rearrange("p c q -> p (c q)"), banks[r % 2]).then_inc(high_done, 1)

            def relu(i, r, first=False):
                g = U * i + r
                act.wait_ge(hid_done, g + 1)
                if not first:
                    act.wait_ge(y_out, 16 * (g - U + 1))
                nc.scalar.activation(y[:, r], hid[:, r % 2], ACT.Relu, scale=0.5).then_inc(relu_done, 1)

            turned_high(0, 0, first=True)
            for r in range(U):
                turned_high((r + 1) // U, (r + 1) % U, first=(r + 1 < U))
                relu(0, r, first=True)
            with act.Fori(1, G // U) as i:
                for r in range(U):
                    turned_high(i + (r + 1) // U, (r + 1) % U)
                    relu(i, r)
            for r in range(G % U):
                if r + 1 < G % U:
                    turned_high(G // U, r + 1)
                relu(G // U, r)

        @block.vector
        def _(dve):
            for n, (counted, free) in enumerate(((exp_done, SC_CREDIT), (pv_done, PV_CREDIT), (out_done, OUT_CREDIT), (den_done, OUT_CREDIT))):
                dve.memset(diag[:, 0, n:n + 1], 0.0).then_inc(counted, free)
            for b in range(B):
                for t in range(b * QT, (b + 1) * QT):
                    dve.wait_ge(x_in[t], 16)
                    dve.bn_stats(stats[:, t, :], x1[:, t]).then_inc(stat_done, 1)
                    dve.wait_ge(stat_done, b * (2 * QT + 2) + 2 * (t - b * QT) + 1)
                    dve.bn_aggr(mv[:, t, :], stats[:, t, :]).then_inc(stat_done, 1)
                ts = slice(b * QT, (b + 1) * QT)
                dve.wait_ge(std_done, b + 1)
                dve.reciprocal(rstd[:, ts], std[:, ts]).then_inc(stat_done, 1)
                dve.wait_ge(stat_done, b * (2 * QT + 2) + 2 * QT + 1)
                dve.scalar_tensor_tensor(out=nmr[:, ts], in0=mv[:, ts, 0], scalar=-1.0, in1=rstd[:, ts],
                                         op0=ALU.mult, op1=ALU.mult).then_inc(stat_done, 1)
                dve.wait_ge(stat_done, (b + 1) * (2 * QT + 2))
                for t in range(b * QT, (b + 1) * QT):
                    for which, col in enumerate((rstd, nmr)):
                        use = 2 * t + which
                        if use == 0:
                            dve.wait_ge(const0, 10)
                            for counted, free in ((exp_done, SC_CREDIT), (pv_done, PV_CREDIT), (out_done, OUT_CREDIT), (den_done, OUT_CREDIT)):
                                dve.wait_ge(counted, free)
                        if use >= 2:
                            dve.wait_ge(row_full, use - 1)
                        dve.tensor_scalar(diag[:, which], ident[:, :], col[:, t:t + 1], None, ALU.mult)\
                           .then_inc(diag_done, 1)

            def unit(n, which):
                dve.wait_ge(ring_full, place(n, which) + 1)
                full = ring[which % 2]
                if which < MAXU:
                    seen = (KT - QT + 1 + which % QT) * P
                    dve.tensor_reduce(mx[:, which:which + 1], full[:, 0:seen], AX.X, ALU.max)\
                       .then_inc(ring_free, 1)
                else:
                    if not (isinstance(n, int) and n == 0):
                        dve.wait_ge(max_in, 16 * n)
                    dve.tensor_scalar(mrow[:, :], full[0:MAXU, 0:P], -1.0, None, ALU.mult)\
                       .then_inc(ring_free, 2)

            def units(step_n, a, b, **kw):
                flat = [u for rnd in plan(**kw) for u in rnd]
                for k, which in flat[a:b]:
                    unit(step_n + k, which)

            def take_out(n):
                dve.wait_ge(pv_done, PV_CREDIT + KT * (n + 1))
                dve.tensor_copy(attnT[:, bass.ds(n, 1), :].rearrange("p o q -> p (o q)"), num[:, :]).then_inc(out_done, 1)

            EARLY = 1
            dve.wait_ge(const0, 9)
            units(-1, 0, None, prologue=True)
            units(0, 0, EARLY)
            with dve.Fori(0, N - 2) as n:
                units(n, EARLY, None)
                units(n + 1, 0, EARLY)
                take_out(n)
            units(N - 2, EARLY, None, following=False)
            take_out(N - 2)
            take_out(N - 1)

            done = [0]

            def post_step(instruction):
                done[0] += 1
                instruction.then_inc(post, 1)

            for t in range(T):
                dve.wait_ge(back_full, t + 1)
                post_step(dve.reciprocal(rden[:, t, :], banks[6 + t % 2].rearrange("p (h d) -> p h d", d=HD)[:, :, 0]))
                dve.wait_ge(post, done[0])
                post_step(dve.tensor_tensor(att[:, t % 2].rearrange("p (h d) -> p h d", d=HD),
                                            banks[t % 2].rearrange("p (h d) -> p h d", d=HD),
                                            rden[:, t, :].unsqueeze(2).broadcast_to([P, HEADS, HD]), ALU.mult))
                dve.wait_ge(post, done[0])
                post_step(dve.tensor_tensor(x1[:, t], att[:, t % 2], x1[:, t], ALU.add))
                dve.wait_ge(post, done[0])
                post_step(dve.bn_stats(stats[:, t, :], x1[:, t]))
                dve.wait_ge(post, done[0])
                post_step(dve.bn_aggr(mv[:, t, :], stats[:, t, :]))
            dve.wait_ge(norm2_done, 1)
            post_step(dve.reciprocal(rstd[:, :], std[:, :]))
            dve.wait_ge(post, done[0])
            post_step(dve.scalar_tensor_tensor(out=nmr[:, :], in0=mv[:, :, 0], scalar=-1.0, in1=rstd[:, :],
                                               op0=ALU.mult, op1=ALU.mult))
            for t in range(T):
                dve.wait_ge(turn_full, t + 1)
                if t >= 2:
                    dve.wait_ge(gate_full, t - 1)
                dve.tensor_copy(xT[:, t % 2].rearrange("p c q -> p (c q)"), banks[2 + t % 2]).then_inc(turn_done, 1)
            dve.wait_ge(gate_full, T)
            dve.wait_ge(gate_in, 32)
            for t in range(T):
                post_step(dve.tensor_tensor(logit[:, t, :], banks[4][:, t * E:(t + 1) * E], gb[:, :], ALU.add))
            dve.wait_ge(post, done[0])
            for t in range(T):
                post_step(dve.max(top[:, t, :], logit[:, t, :]))
            dve.wait_ge(post, done[0])
            for t in range(T):
                post_step(dve.max_index(topi[:, t, :], top[:, t, :], logit[:, t, :]))
            dve.wait_ge(post, done[0])
            post_step(dve.tensor_copy(topf[:, :, :], topi[:, :, :]))
            dve.wait_ge(post, done[0])
            dve.wait_ge(const, 4)
            dve.wait_ge(slot_const, 9)

            def then(instruction):
                post_step(instruction)
                dve.wait_ge(post, done[0])

            post_step(dve.tensor_tensor(pick[:, :, :, :], topf[:, :, 0:2].unsqueeze(3).broadcast_to([P, T, 2, E]),
                                        iota[:, :].unsqueeze(1).unsqueeze(1).broadcast_to([P, T, 2, E]), ALU.is_equal))
            then(dve.tensor_tensor(before_cmp[:, :, :], iota[:, :].unsqueeze(1).broadcast_to([P, E, E]),
                                   iota[:, :].unsqueeze(2).broadcast_to([P, E, E]), ALU.is_lt))
            then(dve.tensor_tensor(both[:, :, :], pick[:, :, 0, :], pick[:, :, 1, :], ALU.add))
            choice_step.append(done[0])
            dve.wait_ge(rank_full, 1)
            ranks, totals = banks[5][:, 0:T * E], banks[5][:, T * E:(T + 1) * E]
            then(dve.tensor_tensor(tiles_cmp[:, :, :], totals.unsqueeze(2).broadcast_to([P, E, T]),
                                   count_step[:, :].unsqueeze(1).broadcast_to([P, E, T]), ALU.is_gt))
            then(dve.tensor_reduce(tiles[:, :], tiles_cmp[:, :, :], AX.X, ALU.add))
            then(dve.tensor_tensor(base_cmp[:, :, :], before_cmp[:, :, :],
                                   tiles[:, :].unsqueeze(1).broadcast_to([P, E, E]), ALU.mult))
            then(dve.tensor_reduce(base[:, :], base_cmp[:, :, :], AX.X, ALU.add))
            post_step(dve.tensor_tensor(end[:, :], base[:, :], tiles[:, :], ALU.add))
            then(dve.tensor_scalar(base_slot[:, :], base[:, :], float(P), None, ALU.mult))
            then(dve.tensor_tensor(where[:, :, :], ranks.rearrange("p (t e) -> p t e", e=E),
                                   base_slot[:, :].unsqueeze(1).broadcast_to([P, T, E]), ALU.add))
            then(dve.tensor_tensor(prod[:, :, :, :], pick[:, :, :, :],
                                   where[:, :, :].unsqueeze(2).broadcast_to([P, T, 2, E]), ALU.mult))
            then(dve.tensor_reduce(pos[:, :], prod[:, :, :, :].rearrange("p t j e -> p (t j) e"), AX.X, ALU.add))
            then(dve.tensor_tensor(pos_cmp[:, :, :], pos[:, :].unsqueeze(2).broadcast_to([P, C, G]),
                                   tile_step[:, :].unsqueeze(1).broadcast_to([P, C, G]), ALU.is_ge))
            then(dve.tensor_reduce(pos_tile[:, :], pos_cmp[:, :, :], AX.X, ALU.add))
            post_step(dve.scalar_tensor_tensor(out=pos_lane[:, :], in0=pos_tile[:, :], scalar=-float(P), in1=pos[:, :],
                                               op0=ALU.mult, op1=ALU.add))
            then(dve.tensor_tensor(tile_hot[:, :, :], pos_tile[:, :].unsqueeze(2).broadcast_to([P, C, G]),
                                   tile_next[:, :].unsqueeze(1).broadcast_to([P, C, G]), ALU.is_equal))
            post_step(dve.tensor_tensor(tile_id[:, :, :], tile_hot[:, :, :],
                                        choice_id[:, :].unsqueeze(2).broadcast_to([P, C, G]), ALU.mult))
            dve.wait_ge(xn_out, 16 * T)
            for c in range(0, C, 4):
                post_step(dve.tensor_tensor(lane_hot[:, c:c + 4, :], pos_lane[:, c:c + 4].unsqueeze(2).broadcast_to([P, 4, P]),
                                            lane[:, :].unsqueeze(1).broadcast_to([P, 4, P]), ALU.is_equal))
                hot_step.append(done[0])
            then(dve.tensor_tensor(owner_cmp[:, :, :], tile_next[:, :].unsqueeze(2).broadcast_to([P, G, E]),
                                   end[:, :].unsqueeze(1).broadcast_to([P, G, E]), ALU.is_gt))
            then(dve.tensor_reduce(owner[:, :], owner_cmp[:, :, :], AX.X, ALU.add))
            post_step(dve.tensor_scalar(owner_id[:, :], owner[:, :], float(E - 1), None, ALU.min))
            owner_step.append(done[0])
            dve.wait_ge(ids_full, 1)
            ids = banks[6][:, 0:G]
            post_step(dve.tensor_scalar(dump[:, :], ids, 0.0, spare_row[:, 0:1], ALU.is_equal, ALU.mult))
            post_step(dve.tensor_scalar(back[:, :], ids, float(B * SQ) + 0.5, -float(B * SQ), ALU.is_gt, ALU.mult))
            then(dve.tensor_scalar(flat[:, :], ids, -1.0, 0.0, ALU.add, ALU.max))
            dve.scalar_tensor_tensor(out=y_row[:, :], in0=ids, scalar=-1.0, in1=dump[:, :],
                                     op0=ALU.add, op1=ALU.add).then_inc(rows_done, 1)
            dve.tensor_tensor(x_row[:, :], flat[:, :], back[:, :], ALU.add).then_inc(rows_done, 1)

            def turned_low(r, i):
                g = U * i + r
                dve.wait_ge(high_done, g + 1)
                dve.tensor_tensor(x_lo[:, r % 2].rearrange("p c q -> p (c q)"), banks[r % 2],
                                  x_hi[:, r % 2].bitcast(F32).rearrange("p c q -> p (c q)"), ALU.subtract)\
                   .then_inc(low_done, 1)

            def add_bias(i, r, first=False):
                g = U * i + r
                e = dve.value_load(owner_id[0:1, bass.ds(g, 1)], min_val=0, max_val=E - 1)
                dve.wait_ge(y_full, g + 1)
                if not (first and r < 2):
                    dve.wait_ge(relu_done, g - 1)
                dve.tensor_tensor(hid[:, r % 2], banks[2 + r], eb[:, bass.ds(e, 1), :].rearrange("p o n -> p (o n)"),
                                  ALU.add).then_inc(hid_done, 1)

            dve.wait_ge(bias_in, 16 * E)
            dve.wait_ge(post, done[0])
            turned_low(0, 0)
            for r in range(U):
                turned_low((r + 1) % U, (r + 1) // U)
                add_bias(0, r, first=True)
            with dve.Fori(1, G // U) as i:
                for r in range(U):
                    turned_low((r + 1) % U, i + (r + 1) // U)
                    add_bias(i, r)
            for r in range(G % U):
                if r + 1 < G % U:
                    turned_low(r + 1, G // U)
                add_bias(G // U, r)

            for t in range(0, T, 2):
                dve.wait_ge(chosen_in[t], 16)
                dve.tensor_tensor(x1[:, t], x1[:, t], chosen[:, t, 0], ALU.add).then_inc(sum_done[0], 1)
                dve.wait_ge(sum_done[0], t + 1)
                dve.tensor_tensor(x1[:, t], x1[:, t], chosen[:, t, 1], ALU.add).then_inc(sum_done[0], 1)

        @block.tensor
        def _(pe):
            pe.wait_ge(const, 3)
            pe.wait_ge(const0, 10)

            for use in range(2 * T):
                t, which = use // 2, use % 2
                pe.wait_ge(diag_done, use + 1)
                pe.matmul(banks[ROW_BANK[t // QT][which]][:, (t % QT) * P:(t % QT + 1) * P], ones[:, :],
                          diag[:, which], start=True, stop=True).then_inc(row_full, 1)
            pe.wait_ge(row_done, 2 * B)

            def unit(i, r, which):
                n = R * i + r
                to = ring[which % 2]
                if which == MAXU:
                    pe.wait_ge(ring_free, place(n, which))
                    pe.transpose(to[:, 0:P], mx[:, :], ident[:, :]).then_inc(ring_full, 2)
                    return
                if not (isinstance(n, int) and place(n, which) < 2):
                    pe.wait_ge(ring_free, place(n, which) - 1)
                if which == 0:
                    pe.wait_ge(kst_in, 16 * COPIES * (n + 1))
                    pe.wait_ge(qst_in, 16 * (COPIES + 1) * (n + 1))
                j, t = which // QT, which % QT
                q = qst[:, r, j, t * P:(t + 1) * P]
                seen = (KT - QT + 1 + t) * P
                pe.matmul(to[:, 0:512], q, kst[:, r, j, 0:512], start=True, stop=True)
                pe.matmul(to[:, 512:seen], q, kst[:, r, j, 512:seen], start=True, stop=False)
                pe.matmul(to[:, seen - P:seen], identb[:, :], mask_qk[:, :], start=False, stop=True)\
                  .then_inc(ring_full, 1)

            def score(i, r, k, j):
                n = R * i + r
                c = ROUND[k]
                place = HG * (KT * n + k) + j
                pe.wait_ge(exp_done, place + 1)
                if k == 0 and j == 0:
                    pe.wait_ge(max_in, 16 * (n + 1))
                q0 = q_from(c)
                masked = c >= KT - QT
                last = pe.matmul(sc[j % 2][:, q0:], kst[:, r, j, c * P:(c + 1) * P],
                                 qst[:, r, j, q0:], start=True, stop=not masked)
                if masked:
                    last = pe.matmul(sc[j % 2][:, q0:q0 + P], identb[:, :], mask_kq[:, :], start=False, stop=True)
                last.then_inc(sc_full, 1)

            def add_round(i, r, k, weighted):
                n = R * i + r
                c = ROUND[k]
                q0 = q_from(c)
                if weighted:
                    pe.wait_ge(exp_done, SC_CREDIT + HG * (KT * n + k + 1))
                if k == 0 and weighted:
                    pe.wait_ge(val_in[r], 16 * (i + 1))
                    pe.wait_ge(out_done, OUT_CREDIT + n)
                if k == 0 and not weighted:
                    pe.wait_ge(den_done, OUT_CREDIT + n)
                for j in range(HG):
                    heads = slice(j * HD, (j + 1) * HD)
                    last = pe.matmul((num if weighted else den)[heads, q0:],
                                     val[:, r, c, heads] if weighted else ones[:, 0:HD], prob[:, k % NP, j, q0:],
                                     start=(k == 0), stop=(k == KT - 1), tile_position=(0, j * HD))
                if not weighted:
                    last.then_inc(pv_done, 1)

            def step(i, r, scores=True, maxima=True, last=False, **kw):
                for k in range(KT):
                    todo = plan(**kw)[k] if maxima else []
                    nxt = (i, r, k + 1) if k + 1 < KT else (*at(i, r, 1), 0) if not last else None
                    for j in range(HG):
                        if scores and nxt:
                            score(*nxt, j)
                        for ahead, which in todo[j:j + 1] if scores else todo if j == 0 else []:
                            unit(*at(i, r, ahead), which)
                        if scores and j in (1, 2):
                            add_round(i, r, k, weighted=(j == 1))

            pe.wait_ge(one_in, 3 * 16 * R)
            step(-1, 2, scores=False, prologue=True)
            for j in range(HG):
                score(0, 0, 0, j)
            with pe.Fori(0, LOOPS) as i:
                for r in range(R):
                    step(i, r)
            step(LOOPS, 0, following=False)
            step(LOOPS, 1, maxima=False, last=True)

            pe.wait_ge(out_done, OUT_CREDIT + N)
            pe.wait_ge(den_done, OUT_CREDIT + N)
            for t in range(T):
                if t >= 2:
                    pe.wait_ge(post, BACK * (t - 2) + 3)
                b, q = t // QT, t % QT
                for g in range(NG):
                    pe.transpose(banks[t % 2][:, g * P:(g + 1) * P],
                                 attnT[:, b * NG + g, q * P:(q + 1) * P], ident[:, :])
                    last = pe.transpose(banks[6 + t % 2][:, g * P:(g + 1) * P],
                                        denT[:, b * NG + g, q * P:(q + 1) * P], ident[:, :])
                last.then_inc(back_full, 1)
            pe.wait_ge(gate_in, 32)
            for t in range(T + 1):
                if t < T:
                    pe.wait_ge(norm2_done, t + 2)
                    if t >= 2:
                        pe.wait_ge(turn_done, t - 1)
                    for c in range(KC):
                        last = pe.transpose(banks[2 + t % 2][:, c * P:(c + 1) * P], xn2[:, t, c * P:(c + 1) * P],
                                            ident[:, :])
                    last.then_inc(turn_full, 1)
                if t >= 1:
                    pe.wait_ge(turn_done, t)
                    for c in range(KC):
                        last = pe.matmul(banks[4][:, (t - 1) * E:t * E], xT[:, (t - 1) % 2, c, :], gw[:, c, :],
                                         start=(c == 0), stop=(c == KC - 1))
                    last.then_inc(gate_full, 1)

            pe.wait_ge(slot_const, 3)
            pe.wait_ge(post, choice_step[0])
            pe.matmul(banks[5][:, 0:T * E], upper[:, :], both[:, :, :].rearrange("p t e -> p (t e)"), start=True, stop=False)
            for t in range(T - 1):
                pe.matmul(banks[5][:, (t + 1) * E:T * E].rearrange("p (s e) -> p s e", e=E), ones_b[:, :],
                          both[:, t:t + 1, :].broadcast_to([P, T - 1 - t, E]), start=False, stop=(t == T - 2))
            for t in range(T):
                last = pe.matmul(banks[5][:, T * E:(T + 1) * E], ones_b[:, :], both[:, t, :],
                                 start=(t == 0), stop=(t == T - 1))
            last.then_inc(rank_full, 1)
            for c in range(C):
                if c % 4 == 0:
                    pe.wait_ge(post, hot_step[c // 4])
                last = pe.matmul(banks[6][:, 0:G], lane_hot[:, c, :], tile_id[:, c, :], start=(c == 0), stop=(c == C - 1))
            last.then_inc(ids_full, 1)

            def turn(i, r, first=False):
                g = U * i + r
                pe.wait_ge(xg_in[r], 16 * (i + 1))
                if not (first and r < 2):
                    pe.wait_ge(low_done, g - 1)
                for c in range(KC):
                    last = pe.transpose(banks[r % 2][:, c * P:(c + 1) * P], xg[:, r, c * P:(c + 1) * P], ident[:, :])
                last.then_inc(tr_full, 1)

            def product(i, r, first=False):
                g = U * i + r
                e = pe.value_load(owner_id[0:1, bass.ds(g, 1)], min_val=0, max_val=E - 1)
                pe.wait_ge(low_done, g + 1)
                if not first:
                    pe.wait_ge(hid_done, g - U + 1)
                for c in range(KC):
                    for k, (a, w) in enumerate(((x_hi, w_hi), (x_hi, w_lo), (x_lo, w_hi))):
                        last = pe.matmul(banks[2 + r], a[:, r % 2, c, :],
                                         w[:, bass.ds(e, 1), c, :].rearrange("p o n -> p (o n)"),
                                         start=(c == 0 and k == 0), stop=(c == KC - 1 and k == 2))
                last.then_inc(y_full, 1)

            pe.wait_ge(w_low, E)
            pe.wait_ge(post, owner_step[0])
            turn(0, 0, first=True)
            for r in range(U):
                turn((r + 1) // U, (r + 1) % U, first=(r + 1 < U))
                product(0, r, first=True)
            with pe.Fori(1, G // U) as i:
                for r in range(U):
                    turn(i + (r + 1) // U, (r + 1) % U)
                    product(i, r)
            for r in range(G % U):
                if r + 1 < G % U:
                    turn(G // U, r + 1)
                product(G // U, r)


_INS = ['x', 'x_T', 'ctx', 'ctx_T', 'L0_ffn_gate_w', 'L0_ffn_gate_b', 'L0_ffn_expert_w', 'L0_ffn_expert_b']
_OUTS = [((2, 512, 512), 'float32')]


def kernel(**inputs):
    import numpy as _np
    import concourse.bacc as _bacc
    from concourse import mybir as _mybir
    from concourse.bass_utils import run_bass_kernel_spmd as _run

    nc = _bacc.Bacc("TRN2", target_bir_lowering=False, num_devices=1)
    arrays, args = {}, []
    x, ctx = _np.asarray(inputs['x']), _np.asarray(inputs['ctx_2048'])
    b, sq, d = x.shape
    sk = ctx.shape[1]
    inputs['x_T'] = x.transpose(0, 2, 1).reshape(b * d // P, P, sq)
    inputs['ctx_T'] = ctx.transpose(0, 2, 1).reshape(b * d // P, P, sk)
    inputs['ctx'] = ctx.reshape(b, sk, d // P, P).transpose(0, 2, 1, 3).reshape(b * d // P, sk, P)
    for name in _INS:
        a = _np.ascontiguousarray(inputs[name])
        arrays[f"in_{name}_dram"] = a
        args.append(nc.dram_tensor(f"in_{name}_dram", a.shape, _mybir.dt.from_np(a.dtype), kind="ExternalInput").ap())
    for i, (shape, dtype) in enumerate(_OUTS):
        dt = _mybir.dt.from_np(_np.dtype(dtype))
        args.append(nc.dram_tensor(f"out_{i}_dram", shape, dt, kind="ExternalOutput").ap())
    args.append(nc.dram_tensor("xn_rows", (b * sq, d), _mybir.dt.float32, kind="Internal").ap())
    args.append(nc.dram_tensor("y_rows", (2 * b * sq + P, d), _mybir.dt.float32, kind="Internal").ap())
    bass_cross_attention_moe(nc, *args)
    r = _run(nc, [arrays], core_ids=[0])
    got = tuple(r.results[0][f"out_{i}_dram"] for i in range(len(_OUTS)))
    return got[0]
```

```python
import concourse.bass as bass
from concourse import mybir
from contextlib import ExitStack

F32 = mybir.dt.float32
F32R = mybir.dt.float32r
BF16 = mybir.dt.bfloat16
U32 = mybir.dt.uint32
I32 = mybir.dt.int32
F16 = mybir.dt.float16
ALU = mybir.AluOpType
ACT = mybir.ActivationFunctionType
AX = mybir.AxisListType

P = 128
HEADS = 16
NEG = -1e30
EPS = 1e-5


def bass_cross_attention_moe(nc, x, x_T, ctx, ctx_T, gate_w, gate_b, expert_w, expert_b, out,
                              xn_rows, y_rows):
    B, SQ, D = x.shape
    SK = ctx.shape[1]
    E = gate_w.shape[1]
    HD = D // HEADS
    HG = P // HD
    NG = D // P
    N = B * NG
    QT = SQ // P
    KT = SK // P
    T = B * QT
    KC = D // P
    SCALE = float(HD) ** -0.5
    ROWS = 3 * HD
    R = 3
    NP = 4
    PAIRS = KT // 2
    SPLITS = 6
    MAXU = HG * QT
    UNITS = MAXU + 2
    COPIES = 3 * HG
    ROUND = [0] + list(range(KT - QT + 1, KT)) + list(range(1, KT - QT + 1))
    AHEAD = 4
    PLAN = [2, 2, 2, 2, 2, 2, 2, 3]
    IN_ROUND = ("score unit score num unit score unit score unit den".split(),
                "score unit score unit score unit score unit num den".split())
    AT_Q, AT_K = 2, 4
    LOOPS = (N - 2) // R
    C = 2 * T
    G = C + E - 1
    U = 4
    EARLY_W = 3
    ORDER = [*range(E - 2), E - 1, E - 2]
    assert B * SQ <= 2048
    assert (B, SQ, SK, HD, HG) == (2, 512, 1024, 32, 4) and (N - 2) % R == 0 and UNITS % 2 == 0

    def q_from(c):
        return max(0, c - (KT - QT)) * P

    def in_attnT(n):
        return n + NG * (n // NG)

    def at(i, r, k):
        return i + (r + k) // R, (r + k) % R

    def query_dmas(n):
        return 16 * ((COPIES + 1) * n - 2 * HG)

    def place(n, which):
        return UNITS * n + which

    def plan(following=True):
        units = [(1, w) for w in range(AHEAD, MAXU + 1)]
        if following:
            units += [(2, w) for w in range(AHEAD)]
        rounds, k = [], 0
        for c in PLAN:
            rounds.append(units[k:k + c])
            k += c
        rounds[-1] += units[k:]
        return rounds

    outer = ExitStack()
    with outer:
        def tensor(stack, name, shape, dt=F32):
            return stack.enter_context(nc.sbuf_tensor(name, shape, dt))

        def sem(name):
            return outer.enter_context(nc.semaphore(name))

        def sems(name):
            return [sem(f"{name}{r}") for r in range(R)]

        ident = tensor(outer, "ident", [P, P])
        identb = tensor(outer, "identb", [P, P], BF16)
        mask_qk = tensor(outer, "mask_qk", [P, P], BF16)
        mask_kq = tensor(outer, "mask_kq", [P, P], BF16)
        ones = tensor(outer, "ones", [P, P])
        stats = tensor(outer, "stats", [P, T, 6])
        mv = tensor(outer, "mv", [P, T, 2])
        std = tensor(outer, "std", [P, T])
        rstd = tensor(outer, "rstd", [P, T])
        nmr = tensor(outer, "nmr", [P, T])
        eps = tensor(outer, "eps", [P, 1])
        x1 = tensor(outer, "x1", [P, T, D])
        gw = tensor(outer, "gw", [P, KC, E])
        gb = tensor(outer, "gb", [E, 1])
        iota = tensor(outer, "iota", [P, E])

        inner = ExitStack()
        attnT = tensor(inner, "attnT", [P, 2 * N, SQ])
        kst, qst = [None] * R, [None] * R
        prob = tensor(inner, "prob", [P, NP, HG, SQ])
        kst[0] = tensor(inner, "kst0", [P, HG, SK], F32R)
        kst[2] = tensor(inner, "kst2", [P, HG, SK], F32R)
        qst[2] = tensor(inner, "qst2", [P, HG, SQ], F32R)
        k_raw = tensor(inner, "k_raw", [P, SK])
        k_hi = tensor(inner, "k_hi", [P, SK], F32R)
        k_lo = tensor(inner, "k_lo", [P, SK], F32R)
        rstd_row = tensor(inner, "rstd_row", [P, T, P])
        nmr_row = tensor(inner, "nmr_row", [P, T, P])
        x_raw = tensor(inner, "x_raw", [P, SQ])
        qn = tensor(inner, "qn", [P, SQ])
        q_hi = tensor(inner, "q_hi", [P, SQ], F32R)
        q_lo = tensor(inner, "q_lo", [P, SQ], F32R)
        kst[1] = tensor(inner, "kst1", [P, HG, SK], F32R)
        qst[0] = tensor(inner, "qst0", [P, HG, SQ], F32R)
        qst[1] = tensor(inner, "qst1", [P, HG, SQ], F32R)
        val = tensor(inner, "val", [P, R, KT, P])
        diag = tensor(inner, "diag", [P, 2, P])
        mx = tensor(inner, "mx", [P, P])
        zeros = tensor(inner, "zeros", [MAXU, P])
        mrow = tensor(inner, "mrow", [MAXU, P], F32R)
        blank = prob[:, 2:4].rearrange("p b j q -> p (b j q)")
        inner.close()

        late = ExitStack()
        w = tensor(late, "w", [P, E, 2, KC, D], F32R)
        eb = tensor(late, "eb", [P, E, D])
        logitT = tensor(late, "logitT", [E, T, P])
        top = tensor(late, "top", [P, T, 8])
        topi = tensor(late, "topi", [P, T, 8], U32)
        topf = tensor(late, "topf", [P, T, 8])
        rden = tensor(late, "rden", [P, T, HEADS])
        pick = tensor(late, "pick", [P, T, 2, E])
        both = tensor(late, "both", [P, T, E], BF16)
        where = tensor(late, "where", [P, T, E])
        prod = tensor(late, "prod", [P, T, 2, E])
        tiles_cmp = tensor(late, "tiles_cmp", [P, E, T])
        tiles = tensor(late, "tiles", [P, E])
        before_cmp = tensor(late, "before_cmp", [P, E, E])
        base_cmp = tensor(late, "base_cmp", [P, E, E])
        base = tensor(late, "base", [P, E])
        base_slot = tensor(late, "base_slot", [P, E])
        end = tensor(late, "end", [P, E])
        owner_cmp = tensor(late, "owner_cmp", [P, G, E])
        owner = tensor(late, "owner", [P, G])
        owner_up = tensor(late, "owner_up", [P, G])
        owner_place = tensor(late, "owner_place", [P, G], I32)
        pos = tensor(late, "pos", [P, C])
        y_row = tensor(late, "y_row", [P, C], I32)
        tile_int = tensor(late, "tile_int", [P, C], I32)
        pos_tile = tensor(late, "pos_tile", [P, C])
        pos_lane = tensor(late, "pos_lane", [P, C])
        tile_hot = tensor(late, "tile_hot", [P, C, G])
        tile_id = tensor(late, "tile_id", [P, C, G], F16)
        x_row = tensor(late, "x_row", [P, G], I32)
        count_step = tensor(late, "count_step", [P, T])
        tile_no = tensor(late, "tile_no", [P, G])
        lane = tensor(late, "lane", [P, P])
        token = tensor(late, "token", [P, C])
        upper = tensor(late, "upper", [P, P], BF16)
        ones_b = tensor(late, "ones_b", [P, P], BF16)
        gating = ExitStack()
        xn2 = tensor(gating, "xn2", [P, T, D])
        xT = tensor(gating, "xT", [P, 2, KC, P])
        att = tensor(gating, "att", [P, 2, D])
        gating.close()
        turning = ExitStack()
        x_hi = tensor(turning, "x_hi", [P, 2, KC, P], F32R)
        x_lo = tensor(turning, "x_lo", [P, 2, KC, P], F32R)
        xg = tensor(turning, "xg", [P, U, D])
        hid = tensor(turning, "hid", [P, 2, D])
        y = tensor(turning, "y", [P, U, D])
        turning.close()
        lane_hot = tensor(late, "lane_hot", [P, C, P], F16)
        late.close()

        final = ExitStack()
        chosen = tensor(final, "chosen", [P, T, 2, D])
        final.close()

        ring = [outer.enter_context(nc.psum_tensor(f"ring{s}", [P, 2 * 512], F32)) for s in range(2)]
        sc = [outer.enter_context(nc.psum_tensor(f"sc{s}", [P, 512], F32)) for s in range(2)]
        num = outer.enter_context(nc.psum_tensor("num", [P, 512], F32))
        den = outer.enter_context(nc.psum_tensor("den", [P, 512], F32))
        banks = [ring[0][:, 0:512], ring[0][:, 512:1024], ring[1][:, 0:512], ring[1][:, 512:1024],
                 sc[0][:, :], sc[1][:, :], num[:, :], den[:, :]]

        ROW_BANK = ((6, 7), (4, 5))

        LOGIT_PARTS = [(5, 0, T // 2), (6, T // 2, T - 1), (0, T - 1, T)]
        logits = [banks[bank][:, t * E:(t + 1) * E] for bank, t0, t1 in LOGIT_PARTS for t in range(t0, t1)]

        SC_CREDIT, PV_CREDIT, OUT_CREDIT = 2, NP // 2, 1
        const0 = sem("const0")
        const = sem("const")
        one_in = sems("one_in")
        x_in = [sem(f"x_in{t}") for t in range(T)]
        stat_done = sem("stat_done")
        std_done = sem("std_done")
        diag_done = sem("diag_done")
        row_full = sem("row_full")
        row_done = sem("row_done")
        kraw_in, xraw_in = sem("kraw_in"), sem("xraw_in")
        val_in = sems("val_in")
        split_done = sem("split_done")
        kst_in, qst_in = sem("kst_in"), sem("qst_in")
        q0_done = sem("q0_done")
        max_in = sem("max_in")
        ring_full = sem("ring_full")
        ring_free = sem("ring_free")
        sc_full = sem("sc_full")
        exp_done = sem("exp_done")
        num_done = sem("num_done")
        add_done = sem("add_done")
        pv_done = sem("pv_done")
        den_done = sem("den_done")
        out_done = sem("out_done")
        CREDITS = ((exp_done, SC_CREDIT), (pv_done, PV_CREDIT), (out_done, OUT_CREDIT), (den_done, OUT_CREDIT))
        gate_in = sem("gate_in")
        bias_in = sem("bias_in")
        back_full = sem("back_full")
        rden_done = sem("rden_done")
        att_done = sem("att_done")
        res_done = sem("res_done")
        bn_done = sem("bn_done")
        mean_done = sem("mean_done")
        std2_done = sem("std2_done")
        rstd2_done = sem("rstd2_done")
        nmr2_done = sem("nmr2_done")
        norm2_done = sem("norm2_done")
        turn_full = sem("turn_full")
        turn_done = sem("turn_done")
        gate_full = sem("gate_full")
        gate_done = sem("gate_done")
        logit_full = sem("logit_full")
        top_done = sem("top_done")
        topi_done = sem("topi_done")
        post = sem("post")
        w_in = [sem(f"w_in{e}") for e in range(E)]
        w_high = sem("w_high")
        w_low = [sem("w_low_pool"), sem("w_low_dve")]
        slot_const = sem("slot_const")
        xn_out = sem("xn_out")
        rank_full = sem("rank_full")
        ids_full = sem("ids_full")
        before_done = sem("before_done")
        both_done = sem("both_done")
        tile_id_done = sem("tile_id_done")
        hot_done = sem("hot_done")
        y_row_done = sem("y_row_done")
        x_row_done = sem("x_row_done")
        owner_done = sem("owner_done")
        xg_in = [sem(f"xg_in{r}") for r in range(U)]
        tr_full = sem("tr_full")
        high_done = sem("high_done")
        low_done = sem("low_done")
        y_full = sem("y_full")
        hid_done = sem("hid_done")
        relu_done = sem("relu_done")
        y_out = [sem(f"y_out{r}") for r in range(U)]
        chosen_in = [sem(f"chosen_in{t}") for t in range(T)]
        sum_done = sem("sum_done")
        stored = sem("stored")

        x_tiles = x.rearrange("b (t p) d -> p (b t) d", p=P)
        out_tiles = out.rearrange("b (t p) d -> p (b t) d", p=P)

        xn_tiles = xn_rows.rearrange("(t p) d -> p t d", p=P)
        y_tiles = y_rows.rearrange("(g p) d -> p g d", p=P)

        block = outer.enter_context(nc.Block())

        @block.sync
        def _(sp):
            def stack(r, n):
                if isinstance(n, int) and n < 2:
                    sp.wait_ge(split_done, SPLITS * n + 1)
                else:
                    sp.wait_ge(exp_done, SC_CREDIT + HG * KT * (n - 2) + 1)
                for to, half in ((0, k_hi), (1, k_hi), (2, k_lo)):
                    if to == 2:
                        sp.wait_ge(split_done, SPLITS * n + 2)
                    for j in range(HG):
                        sp.dma_start(kst[r][to * HD:(to + 1) * HD, j, :].bitcast(F32),
                                     half[j * HD:(j + 1) * HD, :].bitcast(F32)).then_inc(kst_in, 16)
                sp.wait_ge(split_done, SPLITS * n + (5 if isinstance(n, int) else SPLITS))
                sp.dma_start(qst[r][ROWS:ROWS + 1].bitcast(F32).rearrange("o j (t q) -> o (j t) q", q=P),
                             zeros[:, :]).then_inc(qst_in, 16)
                for to, half in ((0, q_hi), (2, q_hi), (1, q_lo))[0:1 if isinstance(n, int) and n == 0 else 3]:
                    if to == 1 and isinstance(n, int):
                        sp.wait_ge(split_done, SPLITS * (n + 1))
                    for j in range(HG):
                        sp.dma_start(qst[r][to * HD:(to + 1) * HD, j, :].bitcast(F32),
                                     half[j * HD:(j + 1) * HD, :].bitcast(F32)).then_inc(qst_in, 16)

            def send_max(r, taken):
                sp.wait_ge(ring_free, taken)
                sp.dma_start(qst[r][ROWS:ROWS + 1].bitcast(F32).rearrange("o j (t q) -> o (j t) q", q=P),
                             mrow[:, :].bitcast(F32)).then_inc(max_in, 16)

            def load_values(r, n):
                sp.dma_start(val[:, r], ctx[bass.ds(n, 1)].rearrange("o (c p) d -> p (o c) d", p=P)).then_inc(val_in[r], 16)

            def step(i, r):
                n = R * i + r
                load_values((r + 1) % R, n + 1)
                stack((r + 2) % R, n + 2)
                send_max((r + 1) % R, UNITS * (n + 2))

            sp.dma_start(k_raw[:, :], ctx_T[0]).then_inc(kraw_in, 16)
            for t in range(T):
                sp.dma_start(x1[:, t], x_tiles[:, t]).then_inc(x_in[t], 16)
                if t == QT - 1:
                    sp.dma_start(x_raw[:, :], x_T[0]).then_inc(xraw_in, 16)
            sp.wait_ge(const0, 9)

            def fill_rest(r):
                sp.dma_start(kst[r][ROWS:ROWS + 1].bitcast(F32).rearrange("o j (t k) -> o (j t) k", k=P),
                             ones[0:HG * KT, :]).then_inc(one_in[r], 16)
                sp.dma_start(kst[r][ROWS + 1:P].bitcast(F32).rearrange("p j s -> p (j s)"),
                             blank[0:P - ROWS - 1, :]).then_inc(one_in[r], 16)
                sp.dma_start(qst[r][ROWS + 1:P].bitcast(F32).rearrange("p j s -> p (j s)"),
                             blank[0:P - ROWS - 1, 0:HG * SQ]).then_inc(one_in[r], 16)

            fill_rest(0)
            stack(0, 0)
            fill_rest(1)
            load_values(0, 0)
            fill_rest(2)
            stack(1, 1)
            with sp.Fori(0, LOOPS) as i:
                for r in range(R):
                    step(i, r)
            load_values(1, N - 1)

            def load_weights(e):
                sp.dma_start(w[:, E - 1 - e, 1].bitcast(F32), expert_w[e].rearrange("(c p) n -> p c n", p=P))\
                  .then_inc(w_in[e], 16)

            sp.wait_ge(exp_done, SC_CREDIT + HG * KT * (N - 2))
            sp.wait_ge(kst_in, 16 * COPIES * N)
            sp.wait_ge(qst_in, query_dmas(N))
            for e in range(EARLY_W):
                load_weights(e)
            send_max(1, UNITS * N)
            sp.dma_start(gw[:, :, :], gate_w.rearrange("(c p) e -> p c e", p=P)).then_inc(gate_in, 16)
            sp.dma_start(gb[:, :], gate_b.rearrange("(e o) -> e o", o=1)).then_inc(gate_in, 16)
            sp.wait_ge(exp_done, SC_CREDIT + HG * KT * (N - 1))
            load_weights(EARLY_W)
            sp.wait_ge(pv_done, PV_CREDIT + PAIRS * N)
            for e in range(EARLY_W + 1, E - 2):
                load_weights(e)
            for t in range(T):
                if t in (2, T - 3):
                    sp.wait_ge(back_full, QT if t == 2 else T)
                    load_weights(E - 1 if t == 2 else E - 2)
                sp.wait_ge(norm2_done, t + 1)
                sp.dma_start(xn_tiles[:, t], xn2[:, t]).then_inc(xn_out, 16)
            for e in range(E):
                sp.dma_start(eb[:, E - 1 - e, :], expert_b[e:e + 1, :].broadcast_to([P, D])).then_inc(bias_in, 16)
            for g in range(G):
                sp.wait_ge(relu_done, g + 1)
                sp.dma_start(y_tiles[:, g], y[:, g % U]).then_inc(y_out[g % U], 16)
            for t in range(T):
                sp.wait_ge(sum_done, 2 * (t + 1))
                sp.dma_start(out_tiles[:, t], x1[:, t]).then_inc(stored, 16)
            sp.wait_ge(stored, 16 * T)
            sp.wait_ge(xn_out, 16 * T)

        @block.gpsimd
        def _(pool):
            pool.memset(ident[:, :], 0.0).then_inc(const0, 1)
            pool.memset(mask_qk[:, :], 0.0).then_inc(const0, 1)
            pool.memset(mask_kq[:, :], 0.0).then_inc(const0, 1)
            pool.memset(ones[:, :], 1.0).then_inc(const0, 1)
            pool.memset(eps[:, :], EPS).then_inc(const0, 1)
            pool.memset(mx[:, :], 0.0).then_inc(const0, 1)
            pool.memset(identb[:, :], 0.0).then_inc(const0, 1)
            pool.memset(zeros[:, :], 0.0).then_inc(const0, 1)
            pool.memset(blank[:, :], 0.0).then_inc(const0, 1)
            pool.wait_ge(const0, 9)
            pool.affine_select(out=ident[:, :], in_=ident[:, :], compare_op=ALU.not_equal, fill=1.0,
                               base=0, pattern=[[-1, P]], channel_multiplier=1).then_inc(const0, 1)
            pool.affine_select(out=mask_qk[:, :], in_=mask_qk[:, :], compare_op=ALU.is_ge, fill=NEG,
                               base=0, pattern=[[-1, P]], channel_multiplier=1).then_inc(const, 1)
            pool.affine_select(out=mask_kq[:, :], in_=mask_kq[:, :], compare_op=ALU.is_ge, fill=NEG,
                               base=0, pattern=[[1, P]], channel_multiplier=-1).then_inc(const, 1)
            pool.affine_select(out=identb[:, :], in_=identb[:, :], compare_op=ALU.not_equal, fill=1.0,
                               base=0, pattern=[[-1, P]], channel_multiplier=1).then_inc(const, 1)
            pool.iota(iota[:, :], pattern=[[1, E]], base=0, channel_multiplier=0,
                      allow_small_or_imprecise_dtypes=True).then_inc(const, 1)

            def keys_low(n):
                if not (isinstance(n, int) and n == 0):
                    pool.wait_ge(kst_in, 16 * COPIES * n)
                pool.wait_ge(split_done, SPLITS * n + 1)
                pool.tensor_tensor(k_lo[:, :], k_raw[:, :], k_hi[:, :].bitcast(F32), ALU.subtract).then_inc(split_done, 1)

            def queries_norm(n):
                b = n // NG
                pool.wait_ge(xraw_in, 16 * (n + 1))
                pool.wait_ge(row_done, 2 * B if not isinstance(n, int) else 2 * (b + 1))
                row = [m[:, bass.ds(b * QT, QT), :].rearrange("p t q -> p (t q)") for m in (rstd_row, nmr_row)]
                pool.tensor_tensor(qn[:, :], x_raw[:, :], row[0], ALU.mult).then_inc(split_done, 1)
                pool.wait_ge(split_done, SPLITS * n + 3)
                pool.tensor_tensor(qn[:, :], qn[:, :], row[1], ALU.add).then_inc(split_done, 1)

            def queries_low(n):
                if not (isinstance(n, int) and n == 0):
                    pool.wait_ge(qst_in, query_dmas(n))
                if isinstance(n, int) and n == 1:
                    pool.wait_ge(q0_done, 2 * HG)
                pool.wait_ge(split_done, SPLITS * n + 5)
                pool.tensor_tensor(q_lo[:, :], qn[:, :], q_hi[:, :].bitcast(F32), ALU.subtract).then_inc(split_done, 1)

            def add_pair(n, p):
                q0 = q_from(ROUND[2 * p + 1])
                onto, other = (prob[:, k % NP, :, q0:] for k in (2 * p, 2 * p + 1))
                pool.wait_ge(num_done, KT * n + 2 * p + 1)
                pool.wait_ge(exp_done, SC_CREDIT + HG * (KT * n + 2 * p + 2))
                pool.tensor_tensor(onto, onto, other, ALU.add).then_inc(add_done, 1)

            def step(n, keys=True, queries=True):
                if queries:
                    queries_norm(n + 2)
                add_pair(n, 0)
                if queries:
                    queries_low(n + 2)
                add_pair(n, 1)
                add_pair(n, 2)
                if keys:
                    keys_low(n + 3)
                add_pair(n, 3)

            for n in range(2):
                keys_low(n)
                queries_norm(n)
                queries_low(n)
            keys_low(2)
            with pool.Fori(0, N - R) as n:
                step(n)
            for n in range(N - R, N):
                step(n, keys=False, queries=n + 2 < N)

            def weights_low(k):
                e = ORDER[k]
                pool.wait_ge(w_high, KC * (k + 1))
                high, low = (w[:, E - 1 - e, half].rearrange("p c n -> p (c n)") for half in range(2))
                pool.tensor_tensor(low, low.bitcast(F32), high.bitcast(F32), ALU.subtract).then_inc(w_low[0], 1)

            pool.wait_ge(out_done, OUT_CREDIT + N)
            pool.wait_ge(den_done, OUT_CREDIT + N)
            pool.memset(ones_b[:, :], 1.0).then_inc(slot_const, 1)
            pool.memset(upper[:, :], 1.0).then_inc(slot_const, 1)
            pool.wait_ge(slot_const, 2)
            pool.affine_select(out=upper[:, :], in_=upper[:, :], compare_op=ALU.is_gt, fill=0.0,
                               base=0, pattern=[[1, P]], channel_multiplier=-1).then_inc(slot_const, 1)
            for to, pattern, by_partition in (
                    (count_step[:, :], [[P, T]], 0), (tile_no[:, :], [[1, G]], 0), (lane[:, :], [[1, P]], 0),
                    (token[:, :], [[P, T], [0, 2]], 1)):
                pool.iota(to, pattern=pattern, base=0, channel_multiplier=by_partition,
                          allow_small_or_imprecise_dtypes=True).then_inc(slot_const, 1)

            for k in range(EARLY_W, E):
                weights_low(k)

            def gather(g):
                if g >= U:
                    pool.wait_ge(tr_full, g - U + 1)
                pool.indirect_dma_start(xg[:, g % U], None, xn_rows[:, :],
                                        bass.IndirectOffsetOnAxis(ap=x_row[:, g:g + 1], axis=0)).then_inc(xg_in[g % U], 16)

            pool.wait_ge(x_row_done, 1)
            pool.wait_ge(gate_full, T)
            pool.wait_ge(xn_out, 16 * T)
            for g in range(G):
                gather(g)

            pool.wait_ge(y_row_done, 1)
            for r in range(U):
                pool.wait_ge(y_out[r], 16 * ((G - 1 - r) // U + 1))
            for t in range(T):
                for j in range(2):
                    c = 2 * t + j
                    pool.indirect_dma_start(chosen[:, t, j], None, y_rows[:, :],
                                            bass.IndirectOffsetOnAxis(ap=y_row[:, c:c + 1], axis=0)).then_inc(chosen_in[t], 16)

        @block.scalar
        def _(act):
            def roots(b):
                ts = slice(b * QT, (b + 1) * QT)
                act.wait_ge(stat_done, b * (2 * QT + 2) + 2 * QT)
                nc.scalar.activation(std[:, ts], mv[:, ts, 1], ACT.Sqrt, bias=eps[:, :]).then_inc(std_done, 1)

            def rows(b):
                act.wait_ge(row_full, 2 * QT * (b + 1))
                for which, row in enumerate((rstd_row, nmr_row)):
                    nc.scalar.copy(row[:, b * QT:(b + 1) * QT].rearrange("p t q -> p (t q)"),
                                   banks[ROW_BANK[b][which]]).then_inc(row_done, 1)

            def keys_high(n):
                act.wait_ge(kraw_in, 16 * (n + 1))
                if not (isinstance(n, int) and n == 0):
                    act.wait_ge(kst_in, 16 * COPIES * n)
                    act.wait_ge(split_done, SPLITS * n)
                nc.scalar.copy(k_hi[:, :], k_raw[:, :]).then_inc(split_done, 1)

            def queries_high(n):
                if not (isinstance(n, int) and n == 0):
                    act.wait_ge(qst_in, query_dmas(n))
                if isinstance(n, int) and n == 1:
                    act.wait_ge(q0_done, 2 * HG)
                act.wait_ge(split_done, SPLITS * n + 4)
                nc.scalar.copy(q_hi[:, :], qn[:, :]).then_inc(split_done, 1)

            def load_keys(n):
                act.wait_ge(split_done, SPLITS * (n - 1) + 2)
                act.dma_start(k_raw[:, :], ctx_T[bass.ds(n, 1)].rearrange("o p s -> p (o s)")).then_inc(kraw_in, 16)

            def load_queries(n):
                act.wait_ge(split_done, SPLITS * (n - 1) + 4)
                act.dma_start(x_raw[:, :], x_T[bass.ds(n, 1)].rearrange("o p s -> p (o s)")).then_inc(xraw_in, 16)

            def exps(n, k):
                q0 = q_from(ROUND[k])
                rnd = KT * n + k
                if isinstance(n, int) and n == 0 and k == 2:
                    for r in range(R):
                        act.wait_ge(one_in[r], 3 * 16)
                if k % 2 == 0:
                    act.wait_ge(pv_done, PAIRS * n + k // 2 + 1)
                for j in range(HG):
                    act.wait_ge(sc_full, HG * rnd + j + 1)
                    nc.scalar.activation(prob[:, k % NP, j, q0:], sc[j % 2][:, q0:], ACT.Exp,
                                         scale=SCALE).then_inc(exp_done, 1)

            def take_sums(n):
                act.wait_ge(pv_done, PV_CREDIT + PAIRS * (n + 1))
                nc.scalar.copy(attnT[:, bass.ds(NG + in_attnT(n), 1), :].rearrange("p o q -> p (o q)"), den[:, :]).then_inc(den_done, 1)

            def weights_high(c):
                e = ORDER[c // KC]
                if c % KC == 0:
                    act.wait_ge(w_in[e], 16)
                nc.scalar.copy(w[:, E - 1 - e, 0, c % KC], w[:, E - 1 - e, 1, c % KC].bitcast(F32)).then_inc(w_high, 1)

            def step(n, first=False, keys=True, queries=True, weights={}):
                if keys:
                    load_keys(n + 3)
                for k in range(1, KT):
                    exps(n, k)
                    for c in weights.get(k, ()):
                        weights_high(c)
                    if k == 2 and not first:
                        take_sums(n - 1)
                    if k == AT_Q and queries:
                        queries_high(n + 2)
                    if k == AT_Q and keys:
                        load_queries(n + 3)
                    if k == AT_K and keys:
                        keys_high(n + 3)
                if not (isinstance(n, int) and n == N - 1):
                    exps(n + 1, 0)

            def send_max_0():
                act.wait_ge(ring_free, UNITS)
                act.dma_start(qst[0][ROWS:ROWS + 1].bitcast(F32).rearrange("o j (t q) -> o (j t) q", q=P),
                              mrow[:, :].bitcast(F32)).then_inc(max_in, 16)

            act.wait_ge(const0, 9)
            keys_high(0)
            roots(0)
            rows(0)
            queries_high(0)
            act.wait_ge(split_done, 5)
            for j in range(HG):
                nc.scalar.copy(qst[0][2 * HD:3 * HD, j, :], q_hi[j * HD:(j + 1) * HD, :].bitcast(F32)).then_inc(q0_done, 1)
            roots(1)
            for n in (1, 2):
                load_keys(n)
                load_queries(n)
                keys_high(n)
                if n == 1:
                    queries_high(n)
            rows(1)
            send_max_0()
            nc.scalar.activation(std[:, 0:1], eps[:, :], ACT.Exp)
            exps(0, 0)
            step(0, first=True)
            with act.Fori(1, N - R) as n:
                step(n)
            early = {N - 2: {k: [k - 4] for k in range(4, KT)},
                     N - 1: {**{k: [k + 3] for k in range(1, KT - 1)}, KT - 1: range(KT + 2, KC * EARLY_W)}}
            for n in range(N - R, N):
                step(n, keys=False, queries=n + 2 < N, weights=early.get(n, {}))
            take_sums(N - 1)

            act.wait_ge(pv_done, PV_CREDIT + PAIRS * N)
            for c in range(KC * EARLY_W, KC * (EARLY_W + 1)):
                weights_high(c)
            first = KC * (EARLY_W + 1)
            with_tile = {u: range(first + 2 * (u - 1), first + 2 * u) for u in range(1, T - 1)}
            with_tile[T + 2] = range(first + 2 * (T - 2), KC * E)
            for u in range(T + 3):
                if 0 <= u - 1 < T:
                    t = u - 1
                    act.wait_ge(nmr2_done, t + 1)
                    nc.scalar.activation(xn2[:, t], x1[:, t], ACT.Identity, bias=nmr[:, t:t + 1],
                                         scale=rstd[:, t:t + 1]).then_inc(norm2_done, 1)
                if u < T:
                    act.wait_ge(mean_done, u + 1)
                    nc.scalar.activation(std[:, u:u + 1], mv[:, u, 1:2], ACT.Sqrt, bias=eps[:, :]).then_inc(std2_done, 1)
                if 0 <= u - 2 < T:
                    t = u - 2
                    act.wait_ge(turn_full, t + 1)
                    if t >= 2:
                        act.wait_ge(gate_full, t - 1)
                    nc.scalar.copy(xT[:, t % 2].rearrange("p c q -> p (c q)"), banks[2 + t % 2]).then_inc(turn_done, 1)
                if 0 <= u - 3 < T:
                    t = u - 3
                    act.wait_ge(gate_full, t + 1)
                    act.wait_ge(gate_in, 32)
                    nc.scalar.activation(logitT[:, t, :], banks[4][0:E, (t % 4) * P:(t % 4 + 1) * P], ACT.Identity,
                                         bias=gb[:, :]).then_inc(gate_done, 1)
                for c in with_tile.get(u, ()):
                    weights_high(c)

            def turned_high(i, r, first=False):
                g = U * i + r
                act.wait_ge(tr_full, g + 1)
                if not (first and r < 2):
                    act.wait_ge(y_full, g - 1)
                nc.scalar.copy(x_hi[:, r % 2].rearrange("p c q -> p (c q)"), banks[r % 2]).then_inc(high_done, 1)

            def relu(i, r, first=False):
                g = U * i + r
                act.wait_ge(hid_done, g + 1)
                if not first:
                    act.wait_ge(y_out[r], 16 * i)
                nc.scalar.activation(y[:, r], hid[:, r % 2], ACT.Relu, scale=0.5).then_inc(relu_done, 1)

            turned_high(0, 0, first=True)
            for r in range(U):
                turned_high((r + 1) // U, (r + 1) % U, first=(r + 1 < U))
                relu(0, r, first=True)
            with act.Fori(1, G // U) as i:
                for r in range(U):
                    turned_high(i + (r + 1) // U, (r + 1) % U)
                    relu(i, r)
            for r in range(G % U):
                if r + 1 < G % U:
                    turned_high(G // U, r + 1)
                relu(G // U, r)

        @block.vector
        def _(dve):
            for n, (counted, free) in enumerate(CREDITS):
                dve.memset(diag[:, 0, n:n + 1], 0.0).then_inc(counted, free)

            def diagonal(use):
                t, which = use // 2, use % 2
                if use == 0:
                    dve.wait_ge(const0, 10)
                    for counted, free in CREDITS:
                        dve.wait_ge(counted, free)
                if use >= 2:
                    dve.wait_ge(row_full, use - 1)
                dve.tensor_scalar(diag[:, which], ident[:, :], (rstd, nmr)[which][:, t:t + 1], None, ALU.mult)\
                   .then_inc(diag_done, 1)

            for b in range(B):
                for t in range(b * QT, (b + 1) * QT):
                    dve.wait_ge(x_in[t], 16)
                    dve.bn_stats(stats[:, t, :], x1[:, t]).then_inc(stat_done, 1)
                    dve.wait_ge(stat_done, b * (2 * QT + 2) + 2 * (t - b * QT) + 1)
                    dve.bn_aggr(mv[:, t, :], stats[:, t, :]).then_inc(stat_done, 1)
                if b == 1:
                    dve.wait_ge(split_done, SPLITS)
                    for j in range(HG):
                        dve.tensor_copy(qst[0][HD:2 * HD, j, :], q_lo[j * HD:(j + 1) * HD, :].bitcast(F32)).then_inc(q0_done, 1)
                ts = slice(b * QT, (b + 1) * QT)
                dve.wait_ge(std_done, b + 1)
                dve.reciprocal(rstd[:, ts], std[:, ts]).then_inc(stat_done, 1)
                dve.wait_ge(stat_done, b * (2 * QT + 2) + 2 * QT + 1)
                dve.scalar_tensor_tensor(out=nmr[:, ts], in0=mv[:, ts, 0], scalar=-1.0, in1=rstd[:, ts],
                                         op0=ALU.mult, op1=ALU.mult).then_inc(stat_done, 1)
                dve.wait_ge(stat_done, (b + 1) * (2 * QT + 2))
                if b == 0:
                    for use in range(2 * QT):
                        diagonal(use)

            def unit(n, which):
                dve.wait_ge(ring_full, place(n, which) + 1)
                full = ring[which % 2]
                if which < MAXU:
                    seen = (KT - QT + 1 + which % QT) * P
                    dve.tensor_reduce(mx[:, which:which + 1], full[:, 0:seen], AX.X, ALU.max)\
                       .then_inc(ring_free, 1)
                else:
                    if not (isinstance(n, int) and n == 0):
                        dve.wait_ge(max_in, 16 * n)
                    dve.tensor_scalar(mrow[:, :], full[0:MAXU, 0:P], -1.0, None, ALU.mult)\
                       .then_inc(ring_free, 2)

            def units(step_n, **kw):
                for ring_units in plan(**kw):
                    for k, which in ring_units:
                        unit(step_n + k, which)

            def take_out(n):
                dve.wait_ge(num_done, KT * (n + 1))
                dve.tensor_copy(attnT[:, bass.ds(in_attnT(n), 1), :].rearrange("p o q -> p (o q)"), num[:, :]).then_inc(out_done, 1)

            dve.wait_ge(const0, 9)
            diagonal(2 * QT)
            diagonal(2 * QT + 1)
            for which in range(MAXU + 1):
                unit(0, which)
                if which % 2 == 0 and 1 <= which // 2 < 2 * QT - 1:
                    diagonal(2 * QT + which // 2 + 1)
            for which in range(AHEAD):
                unit(1, which)
            with dve.Fori(0, N - 2) as n:
                units(n)
                take_out(n)
            units(N - 2, following=False)
            take_out(N - 2)

            def weights_low(k):
                dve.wait_ge(w_high, KC * (k + 1))
                high, low = (w[:, E - 1 - ORDER[k], half].rearrange("p c n -> p (c n)") for half in range(2))
                dve.tensor_tensor(low, low.bitcast(F32), high.bitcast(F32), ALU.subtract).then_inc(w_low[1], 1)

            for k in range(EARLY_W - 1):
                weights_low(k)
            take_out(N - 1)
            weights_low(EARLY_W - 1)

            dve.wait_ge(const, 4)
            dve.tensor_tensor(before_cmp[:, :, :], iota[:, :].unsqueeze(1).broadcast_to([P, E, E]),
                              iota[:, :].unsqueeze(2).broadcast_to([P, E, E]), ALU.is_lt).then_inc(before_done, 1)
            for u in range(T + 1):
                if u < T:
                    t = u
                    dve.wait_ge(back_full, t + 1)
                    dve.reciprocal(rden[:, t, :], banks[6 + t % 2].rearrange("p (h d) -> p h d", d=HD)[:, :, 0])\
                       .then_inc(rden_done, 1)
                if 0 <= u - 1 < T:
                    dve.wait_ge(std2_done, u)
                    dve.reciprocal(rstd[:, u - 1:u], std[:, u - 1:u]).then_inc(rstd2_done, 1)
                if u < T:
                    dve.wait_ge(rden_done, t + 1)
                    dve.tensor_tensor(att[:, t % 2].rearrange("p (h d) -> p h d", d=HD),
                                      banks[t % 2].rearrange("p (h d) -> p h d", d=HD),
                                      rden[:, t, :].unsqueeze(2).broadcast_to([P, HEADS, HD]), ALU.mult).then_inc(att_done, 1)
                if 0 <= u - 1 < T:
                    dve.wait_ge(rstd2_done, u)
                    dve.scalar_tensor_tensor(out=nmr[:, u - 1:u], in0=mv[:, u - 1, 0:1], scalar=-1.0,
                                             in1=rstd[:, u - 1:u], op0=ALU.mult, op1=ALU.mult).then_inc(nmr2_done, 1)
                if u < T:
                    dve.wait_ge(att_done, t + 1)
                    dve.tensor_tensor(x1[:, t], att[:, t % 2], x1[:, t], ALU.add).then_inc(res_done, 1)
                if u < T:
                    dve.wait_ge(res_done, t + 1)
                    dve.bn_stats(stats[:, t, :], x1[:, t]).then_inc(bn_done, 1)
                if u < T:
                    dve.wait_ge(bn_done, t + 1)
                    dve.bn_aggr(mv[:, t, :], stats[:, t, :]).then_inc(mean_done, 1)

            for bank, t0, t1 in LOGIT_PARTS:
                dve.wait_ge(logit_full, t1)
                for t in range(t0, t1):
                    dve.max(top[:, t, :], logits[t]).then_inc(top_done, 1)
                for t in range(t0, t1):
                    dve.wait_ge(top_done, t + 1)
                    dve.max_index(topi[:, t, :], top[:, t, :], logits[t]).then_inc(topi_done, 1)
            dve.wait_ge(topi_done, T)
            dve.wait_ge(slot_const, 7)
            dve.wait_ge(before_done, 1)
            done = [0]

            def post_step(instruction):
                done[0] += 1
                instruction.then_inc(post, 1)

            def then(instruction):
                post_step(instruction)
                dve.wait_ge(post, done[0])

            then(dve.tensor_copy(topf[:, :, :], topi[:, :, :]))
            then(dve.tensor_tensor(pick[:, :, :, :], topf[:, :, 0:2].unsqueeze(3).broadcast_to([P, T, 2, E]),
                                        iota[:, :].unsqueeze(1).unsqueeze(1).broadcast_to([P, T, 2, E]), ALU.is_equal))
            dve.tensor_tensor(both[:, :, :], pick[:, :, 0, :], pick[:, :, 1, :], ALU.add).then_inc(both_done, 1)
            dve.wait_ge(rank_full, 1)
            ranks, totals = banks[7][:, 0:T * E], banks[7][:, T * E:(T + 1) * E]
            then(dve.tensor_tensor(tiles_cmp[:, :, :], totals.unsqueeze(2).broadcast_to([P, E, T]),
                                   count_step[:, :].unsqueeze(1).broadcast_to([P, E, T]), ALU.is_gt))
            then(dve.tensor_reduce(tiles[:, :], tiles_cmp[:, :, :], AX.X, ALU.add))
            then(dve.tensor_tensor(base_cmp[:, :, :], before_cmp[:, :, :],
                                   tiles[:, :].unsqueeze(1).broadcast_to([P, E, E]), ALU.mult))
            then(dve.tensor_reduce(base[:, :], base_cmp[:, :, :], AX.X, ALU.add))
            post_step(dve.tensor_tensor(end[:, :], base[:, :], tiles[:, :], ALU.add))
            then(dve.tensor_scalar(base_slot[:, :], base[:, :], float(P), None, ALU.mult))
            then(dve.tensor_tensor(where[:, :, :], ranks.rearrange("p (t e) -> p t e", e=E),
                                   base_slot[:, :].unsqueeze(1).broadcast_to([P, T, E]), ALU.add))
            then(dve.tensor_tensor(prod[:, :, :, :], pick[:, :, :, :],
                                   where[:, :, :].unsqueeze(2).broadcast_to([P, T, 2, E]), ALU.mult))
            then(dve.tensor_reduce(pos[:, :], prod[:, :, :, :].rearrange("p t j e -> p (t j) e"), AX.X, ALU.add))
            dve.tensor_copy(y_row[:, :], pos[:, :]).then_inc(y_row_done, 1)
            dve.wait_ge(y_row_done, 1)
            then(dve.tensor_scalar(tile_int[:, :], y_row[:, :], P.bit_length() - 1, None, ALU.logical_shift_right))
            then(dve.tensor_copy(pos_tile[:, :], tile_int[:, :]))
            post_step(dve.scalar_tensor_tensor(out=pos_lane[:, :], in0=pos_tile[:, :], scalar=-float(P), in1=pos[:, :],
                                               op0=ALU.mult, op1=ALU.add))
            then(dve.tensor_tensor(tile_hot[:, :, :], pos_tile[:, :].unsqueeze(2).broadcast_to([P, C, G]),
                                   tile_no[:, :].unsqueeze(1).broadcast_to([P, C, G]), ALU.is_equal))
            dve.tensor_tensor(tile_id[:, :, :], tile_hot[:, :, :], token[:, :].unsqueeze(2).broadcast_to([P, C, G]),
                              ALU.mult).then_inc(tile_id_done, 1)
            dve.wait_ge(xn_out, 16 * T)
            for c in range(0, C, 4):
                dve.tensor_tensor(lane_hot[:, c:c + 4, :], pos_lane[:, c:c + 4].unsqueeze(2).broadcast_to([P, 4, P]),
                                  lane[:, :].unsqueeze(1).broadcast_to([P, 4, P]), ALU.is_equal).then_inc(hot_done, 1)
            dve.wait_ge(ids_full, 1)
            dve.tensor_copy(x_row[:, :], banks[6][:, 0:G]).then_inc(x_row_done, 1)
            then(dve.tensor_tensor(owner_cmp[:, :, :], tile_no[:, :].unsqueeze(2).broadcast_to([P, G, E]),
                                   end[:, :].unsqueeze(1).broadcast_to([P, G, E]), ALU.is_ge))
            then(dve.tensor_reduce(owner[:, :], owner_cmp[:, :, :], AX.X, ALU.add))
            then(dve.tensor_scalar(owner_up[:, :], owner[:, :], float(E - 1), None, ALU.min))
            dve.tensor_scalar(owner_place[:, :], owner_up[:, :], -1.0, float(E - 1), ALU.mult, ALU.add).then_inc(owner_done, 1)
            def turned_low(i, r):
                g = U * i + r
                dve.wait_ge(high_done, g + 1)
                dve.tensor_tensor(x_lo[:, r % 2].rearrange("p c q -> p (c q)"), banks[r % 2],
                                  x_hi[:, r % 2].bitcast(F32).rearrange("p c q -> p (c q)"), ALU.subtract)\
                   .then_inc(low_done, 1)

            def add_bias(i, r, first=False):
                g = U * i + r
                e = dve.value_load(owner_place[0:1, bass.ds(g, 1)], min_val=0, max_val=E - 1)
                dve.wait_ge(y_full, g + 1)
                if not (first and r < 2):
                    dve.wait_ge(relu_done, g - 1)
                dve.tensor_tensor(hid[:, r % 2], banks[2 + r], eb[:, bass.ds(e, 1), :].rearrange("p o n -> p (o n)"),
                                  ALU.add).then_inc(hid_done, 1)

            dve.wait_ge(bias_in, 16 * E)
            dve.wait_ge(owner_done, 1)
            turned_low(0, 0)
            for r in range(U):
                turned_low((r + 1) // U, (r + 1) % U)
                add_bias(0, r, first=True)
            with dve.Fori(1, G // U) as i:
                for r in range(U):
                    turned_low(i + (r + 1) // U, (r + 1) % U)
                    add_bias(i, r)
            for r in range(G % U):
                if r + 1 < G % U:
                    turned_low(G // U, r + 1)
                add_bias(G // U, r)

            for t in range(T):
                dve.wait_ge(chosen_in[t], 32)
                dve.tensor_tensor(x1[:, t], x1[:, t], chosen[:, t, 0], ALU.add).then_inc(sum_done, 1)
                dve.wait_ge(sum_done, 2 * t + 1)
                dve.tensor_tensor(x1[:, t], x1[:, t], chosen[:, t, 1], ALU.add).then_inc(sum_done, 1)

        @block.tensor
        def _(pe):
            pe.wait_ge(const, 3)
            pe.wait_ge(const0, 10)

            def row(use):
                t, which = use // 2, use % 2
                pe.wait_ge(diag_done, use + 1)
                pe.matmul(banks[ROW_BANK[t // QT][which]][:, (t % QT) * P:(t % QT + 1) * P], ones[:, :],
                          diag[:, which], start=True, stop=True).then_inc(row_full, 1)

            for use in range(2 * QT):
                row(use)

            def unit(i, r, which):
                n = R * i + r
                to = ring[which % 2]
                if which == MAXU:
                    pe.wait_ge(ring_free, place(n, which))
                    pe.transpose(to[:, 0:P], mx[:, :], ident[:, :]).then_inc(ring_full, 2)
                    return
                if not (isinstance(n, int) and place(n, which) < 2):
                    pe.wait_ge(ring_free, place(n, which) - 1)
                if which == 0 and isinstance(n, int) and n == 0:
                    pe.wait_ge(q0_done, 2 * HG)
                if which == 0 and isinstance(n, int) and n < 2:
                    pe.wait_ge(one_in[n], 3 * 16)
                if which == 0:
                    pe.wait_ge(kst_in, 16 * COPIES * (n + 1))
                    pe.wait_ge(qst_in, query_dmas(n + 1))
                j, t = which // QT, which % QT
                q = qst[r][:, j, t * P:(t + 1) * P]
                seen = (KT - QT + 1 + t) * P
                pe.matmul(to[:, 0:512], q, kst[r][:, j, 0:512], start=True, stop=True)
                pe.matmul(to[:, 512:seen], q, kst[r][:, j, 512:seen], start=True, stop=False)
                pe.matmul(to[:, seen - P:seen], identb[:, :], mask_qk[:, :], start=False, stop=True)\
                  .then_inc(ring_full, 1)

            def score(i, r, k, j):
                n = R * i + r
                c = ROUND[k]
                place = HG * (KT * n + k) + j
                pe.wait_ge(exp_done, place + 1)
                if k == 0 and j == 0:
                    pe.wait_ge(max_in, 16 * (n + 1))
                q0 = q_from(c)
                masked = c >= KT - QT
                last = pe.matmul(sc[j % 2][:, q0:], kst[r][:, j, c * P:(c + 1) * P],
                                 qst[r][:, j, q0:], start=True, stop=not masked)
                if masked:
                    last = pe.matmul(sc[j % 2][:, q0:q0 + P], identb[:, :], mask_kq[:, :], start=False, stop=True)
                last.then_inc(sc_full, 1)

            def add_num(i, r, k):
                n = R * i + r
                c = ROUND[k]
                q0 = q_from(c)
                pe.wait_ge(exp_done, SC_CREDIT + HG * (KT * n + k + 1))
                if k == 0:
                    pe.wait_ge(val_in[r], 16 * (i + 1))
                    pe.wait_ge(out_done, OUT_CREDIT + n)
                for j in range(HG):
                    heads = slice(j * HD, (j + 1) * HD)
                    last = pe.matmul(num[heads, q0:], val[:, r, c, heads], prob[:, k % NP, j, q0:],
                                     start=(k == 0), stop=(k == KT - 1), tile_position=(0, j * HD))
                last.then_inc(num_done, 1)

            def add_den(i, r, p):
                n = R * i + r
                k = 2 * p
                q0 = q_from(ROUND[k])
                pe.wait_ge(add_done, PAIRS * n + p + 1)
                if p == 0:
                    pe.wait_ge(den_done, OUT_CREDIT + n)
                for j in range(HG):
                    last = pe.matmul(den[j * HD:(j + 1) * HD, q0:], ones[:, 0:HD], prob[:, k % NP, j, q0:],
                                     start=(p == 0), stop=(p == PAIRS - 1), tile_position=(0, j * HD))
                last.then_inc(pv_done, 1)

            def round_(i, r, k, den=None, maxima=True, last=False, **kw):
                todo = iter(plan(**kw)[k] if maxima else [])
                nxt = (i, r, k + 1) if k + 1 < KT else (*at(i, r, 1), 0) if not last else None
                heads = iter(range(HG))
                for what in IN_ROUND[k % 2]:
                    if what == "score" and nxt:
                        score(*nxt, next(heads))
                    if what == "unit":
                        for ahead, which in [u for u in [next(todo, None)] if u]:
                            unit(*at(i, r, ahead), which)
                    if what == "num":
                        add_num(i, r, k)
                    if what == "den" and den:
                        add_den(*den)
                for ahead, which in todo:
                    unit(*at(i, r, ahead), which)

            def step(i, r, later={}, **kw):
                for k in range(1, KT):
                    round_(i, r, k, den=(i, r, k // 2 - 1) if k % 2 == 0 else None, **kw)
                if not kw.get("last"):
                    round_(*at(i, r, 1), 0, den=(i, r, PAIRS - 1), **later)

            for which in range(MAXU + 1):
                unit(0, 0, which)
                if which % 2 == 1:
                    row(2 * QT + which // 2)
            pe.wait_ge(row_done, 2 * B)
            for j in range(HG):
                score(0, 0, 0, j)
            for which in range(AHEAD):
                unit(0, 1, which)
            pe.wait_ge(one_in[2], 3 * 16)
            round_(0, 0, 0)
            with pe.Fori(0, LOOPS) as i:
                for r in range(R):
                    step(i, r)
            step(LOOPS, 0, following=False, later=dict(maxima=False))
            step(LOOPS, 1, maxima=False, last=True)
            add_den(LOOPS, 1, PAIRS - 1)

            pe.wait_ge(out_done, OUT_CREDIT + N)
            pe.wait_ge(den_done, OUT_CREDIT + N)
            for u in range(T + 4):
                if u < T:
                    t = u
                    if t >= 2:
                        pe.wait_ge(att_done, t - 1)
                    b, q = t // QT, t % QT
                    for g in range(NG):
                        pe.transpose(banks[t % 2][:, g * P:(g + 1) * P],
                                     attnT[:, in_attnT(b * NG + g), q * P:(q + 1) * P], ident[:, :])
                        last = pe.transpose(banks[6 + t % 2][:, g * P:(g + 1) * P],
                                            attnT[:, NG + in_attnT(b * NG + g), q * P:(q + 1) * P], ident[:, :])
                    last.then_inc(back_full, 1)
                if 0 <= u - 2 < T:
                    t = u - 2
                    pe.wait_ge(norm2_done, t + 1)
                    if t >= 2:
                        pe.wait_ge(turn_done, t - 1)
                    for c in range(KC):
                        last = pe.transpose(banks[2 + t % 2][:, c * P:(c + 1) * P], xn2[:, t, c * P:(c + 1) * P],
                                            ident[:, :])
                    last.then_inc(turn_full, 1)
                if 0 <= u - 3 < T:
                    t = u - 3
                    pe.wait_ge(turn_done, t + 1)
                    if t == 0:
                        pe.wait_ge(gate_in, 32)
                    if t >= 1:
                        pe.wait_ge(gate_done, t)
                    for c in range(KC):
                        last = pe.matmul(banks[4][0:E, (t % 4) * P:(t % 4 + 1) * P], gw[:, c, :], xT[:, t % 2, c, :],
                                         start=(c == 0), stop=(c == KC - 1))
                    last.then_inc(gate_full, 1)
                if 0 <= u - 4 < T:
                    t = u - 4
                    pe.wait_ge(gate_done, t + 1)
                    if t == T // 2:
                        pe.wait_ge(att_done, T)
                    pe.transpose(logits[t], logitT[:, t, :], ident[0:E, 0:E]).then_inc(logit_full, 1)

            pe.wait_ge(slot_const, 3)
            pe.wait_ge(both_done, 1)
            pe.matmul(banks[7][:, 0:T * E], upper[:, :], both[:, :, :].rearrange("p t e -> p (t e)"), start=True, stop=False)
            for t in range(T - 1):
                pe.matmul(banks[7][:, (t + 1) * E:T * E].rearrange("p (s e) -> p s e", e=E), ones_b[:, :],
                          both[:, t:t + 1, :].broadcast_to([P, T - 1 - t, E]), start=False, stop=(t == T - 2))
            for t in range(T):
                last = pe.matmul(banks[7][:, T * E:(T + 1) * E], ones_b[:, :], both[:, t, :],
                                 start=(t == 0), stop=(t == T - 1))
            last.then_inc(rank_full, 1)
            pe.wait_ge(tile_id_done, 1)
            for c in range(C):
                if c % 4 == 0:
                    pe.wait_ge(hot_done, c // 4 + 1)
                last = pe.matmul(banks[6][:, 0:G], lane_hot[:, c, :], tile_id[:, c, :], start=(c == 0), stop=(c == C - 1))
            last.then_inc(ids_full, 1)

            def turn(i, r, first=False):
                g = U * i + r
                pe.wait_ge(xg_in[r], 16 * (i + 1))
                if not (first and r < 2):
                    pe.wait_ge(low_done, g - 1)
                for c in range(KC):
                    last = pe.transpose(banks[r % 2][:, c * P:(c + 1) * P], xg[:, r, c * P:(c + 1) * P], ident[:, :])
                last.then_inc(tr_full, 1)

            def product(i, r, first=False):
                g = U * i + r
                e = pe.value_load(owner_place[0:1, bass.ds(g, 1)], min_val=0, max_val=E - 1)
                pe.wait_ge(low_done, g + 1)
                if not first:
                    pe.wait_ge(hid_done, g - U + 1)
                for c in range(KC):
                    for k, (a, half) in enumerate(((x_hi, 0), (x_hi, 1), (x_lo, 0))):
                        last = pe.matmul(banks[2 + r], a[:, r % 2, c, :],
                                         w[:, bass.ds(e, 1), half, c, :].rearrange("p o n -> p (o n)"),
                                         start=(c == 0 and k == 0), stop=(c == KC - 1 and k == 2))
                last.then_inc(y_full, 1)

            turn(0, 0, first=True)
            pe.wait_ge(w_low[0], E - EARLY_W)
            pe.wait_ge(w_low[1], EARLY_W)
            pe.wait_ge(owner_done, 1)
            for r in range(U):
                turn((r + 1) // U, (r + 1) % U, first=(r + 1 < U))
                product(0, r, first=True)
            with pe.Fori(1, G // U) as i:
                for r in range(U):
                    turn(i + (r + 1) // U, (r + 1) % U)
                    product(i, r)
            for r in range(G % U):
                if r + 1 < G % U:
                    turn(G // U, r + 1)
                product(G // U, r)


_INS = ['x', 'x_T', 'ctx', 'ctx_T', 'L0_ffn_gate_w', 'L0_ffn_gate_b', 'L0_ffn_expert_w', 'L0_ffn_expert_b']
_OUTS = [((2, 512, 512), 'float32')]


def kernel(**inputs):
    import numpy as _np
    import concourse.bacc as _bacc
    from concourse import mybir as _mybir
    from concourse.bass_utils import run_bass_kernel_spmd as _run

    nc = _bacc.Bacc("TRN2", target_bir_lowering=False, num_devices=1)
    arrays, args = {}, []
    x, ctx = _np.asarray(inputs['x']), _np.asarray(inputs['ctx_2048'])
    b, sq, d = x.shape
    sk = ctx.shape[1]
    inputs['x_T'] = x.transpose(0, 2, 1).reshape(b * d // P, P, sq)
    inputs['ctx_T'] = ctx.transpose(0, 2, 1).reshape(b * d // P, P, sk)
    inputs['ctx'] = ctx.reshape(b, sk, d // P, P).transpose(0, 2, 1, 3).reshape(b * d // P, sk, P)
    for name in _INS:
        a = _np.ascontiguousarray(inputs[name])
        arrays[f"in_{name}_dram"] = a
        args.append(nc.dram_tensor(f"in_{name}_dram", a.shape, _mybir.dt.from_np(a.dtype), kind="ExternalInput").ap())
    for i, (shape, dtype) in enumerate(_OUTS):
        dt = _mybir.dt.from_np(_np.dtype(dtype))
        args.append(nc.dram_tensor(f"out_{i}_dram", shape, dt, kind="ExternalOutput").ap())
    n_experts = inputs['L0_ffn_gate_w'].shape[1]
    args.append(nc.dram_tensor("xn_rows", (b * sq, d), _mybir.dt.float32, kind="Internal").ap())
    args.append(nc.dram_tensor("y_rows", ((2 * b * sq // P + n_experts - 1) * P, d), _mybir.dt.float32, kind="Internal").ap())
    bass_cross_attention_moe(nc, *args)
    r = _run(nc, [arrays], core_ids=[0])
    got = tuple(r.results[0][f"out_{i}_dram"] for i in range(len(_OUTS)))
    return got[0]
```
